# Optimizing a Trainium2 kernel written in Bass

```python
import numpy as np
import jax
import jax.numpy as jnp

def _softmax(x, axis=-1):
    return jax.nn.softmax(x, axis=axis)

def _gelu(x):
    return jax.nn.gelu(x, approximate=True)

def _silu(x):
    return jax.nn.silu(x)

def _sigmoid(x):
    return jax.nn.sigmoid(x)

def _layernorm(x, axis=-1, eps=1e-05):
    m = jnp.mean(x, axis=axis, keepdims=True)
    v = jnp.var(x, axis=axis, keepdims=True)
    return (x - m) / jnp.sqrt(v + eps)

def _scatter_add(tgt, idx, src, axis=0):
    return tgt.at[idx].add(src)

def _segment_sum(src, seg, n):
    return jax.ops.segment_sum(src, seg, n)
kernel_name = 'mk_adj_preln_d4_adj_r2_2c6823'

def setup_inputs(seed: int=0):
    np.random.seed(seed)
    _w = jnp.asarray

    def _rec_inputs():
        import jax
        import jax.numpy as jnp
        _gk = jax.random.key(seed)
        x = -0.0002928 + 1 * jax.random.normal(jax.random.fold_in(_gk, 1), (4096, 256), jnp.float32)
        _a = jax.random.bernoulli(jax.random.fold_in(_gk, 2), 0.000976562, (4096, 4096))
        _a = jnp.logical_or(_a, jnp.swapaxes(_a, -1, -2))
        _a = jnp.logical_or(_a, jnp.eye(4096, dtype=bool))
        _af = _a.astype(jnp.float32)
        adj = _af
        return (x, adj)
    x, adj = _rec_inputs()

    def _L0_gnn_setup():
        import jax, jax.numpy as jnp
        import numpy as np
        SIZE_U = 2048
        SIZE_V = 2048
        N = SIZE_U + SIZE_V
        C_IN = 256
        C_OUT = 256
        EDGE_P = 0.005
        LEAKY_SLOPE = 0.01

        def _xavier_uniform(key, shape):
            fan_in, fan_out = shape
            lim = float(np.sqrt(6.0 / (fan_in + fan_out)))
            return jax.random.uniform(key, shape, jnp.float32, minval=-lim, maxval=lim)
        key = jax.random.key(seed)
        k1, k2, k3, k4 = jax.random.split(key, 4)
        x = jax.random.normal(k1, (N, C_IN), jnp.float32)
        adj = (jax.random.uniform(k2, (N, N)) < EDGE_P).astype(jnp.float32)
        weightr = _xavier_uniform(k3, (C_IN, C_OUT))
        weightd = _xavier_uniform(k4, (C_IN, C_OUT))
        bias = jnp.zeros((C_OUT,), jnp.float32)
        return {'x': x, 'adj': adj, 'weightr': weightr, 'weightd': weightd, 'bias': bias}
    _L0_gnn_all = _L0_gnn_setup()
    _L0_gnn_in = {k: v for k, v in _L0_gnn_all.items() if k in ('weightr', 'weightd', 'bias')}
    del _L0_gnn_all

    def _L1_gnn_setup():
        import jax, jax.numpy as jnp
        import numpy as np
        EPS = 1e-08
        key = jax.random.key(seed)
        k1, k2, k3, k4 = jax.random.split(key, 4)
        N, IN, OUT = (4096, 256, 256)
        x = jax.random.normal(k1, (N, IN), dtype=jnp.float32)
        adj = jax.random.uniform(k2, (N, N), dtype=jnp.float32)
        W = jax.random.normal(k3, (OUT, IN), dtype=jnp.float32) * (1.0 / np.sqrt(IN))
        b = jax.random.normal(k4, (OUT,), dtype=jnp.float32) * 0.01
        return {'x': x, 'adj': adj, 'W': W, 'b': b}
    _L1_gnn_all = _L1_gnn_setup()
    _L1_gnn_in = {k: v for k, v in _L1_gnn_all.items() if k in ('W', 'b')}
    del _L1_gnn_all

    def _L2_gnn_setup():
        import jax, jax.numpy as jnp
        import numpy as np
        N, NIN, NOUT = (4096, 256, 256)
        key = jax.random.key(seed)
        k1, k2, k3 = jax.random.split(key, 3)
        H = jax.random.normal(k1, (N, NIN), dtype=jnp.float32)
        adj_matrix = jax.random.uniform(k2, (N, N), dtype=jnp.float32)
        W = jax.random.normal(k3, (NOUT, NIN), dtype=jnp.float32) / np.sqrt(NIN)
        b = jnp.zeros((NOUT,), dtype=jnp.float32)
        return {'H': H, 'adj_matrix': adj_matrix, 'W': W, 'b': b}
    _L2_gnn_all = _L2_gnn_setup()
    _L2_gnn_in = {k: v for k, v in _L2_gnn_all.items() if k in ('W', 'b')}
    del _L2_gnn_all

    def _L3_gnn_setup():
        import jax, jax.numpy as jnp
        import numpy as np
        N = 8192
        D_IN = 256
        D_OUT = 256
        AVG_DEG = 32.0
        key = jax.random.key(seed)
        k1, k2, k3, k4 = jax.random.split(key, 4)
        p = AVG_DEG / N
        adjacency = (jax.random.uniform(k1, (N, N)) < p).astype(jnp.float32)
        adjacency = jnp.maximum(adjacency, adjacency.T)
        node_degree = jnp.sum(adjacency, axis=1, keepdims=True) + 1.0
        x = jax.random.normal(k2, (N, D_IN), dtype=jnp.float32)
        W = jax.random.normal(k3, (D_IN, D_OUT), dtype=jnp.float32) * (1.0 / np.sqrt(D_IN))
        b = jax.random.normal(k4, (D_OUT,), dtype=jnp.float32) * 0.01
        return {'x': x, 'adjacency': adjacency, 'node_degree': node_degree, 'W': W, 'b': b}
    _L3_gnn_all = _L3_gnn_setup()
    _L3_gnn_in = {k: v for k, v in _L3_gnn_all.items() if k in ('W', 'b')}
    del _L3_gnn_all
    return {'x': x, 'adj': adj, 'L0_gnn_weightr': _L0_gnn_in['weightr'], 'L0_gnn_weightd': _L0_gnn_in['weightd'], 'L0_gnn_bias': _L0_gnn_in['bias'], 'L1_gnn_W': _L1_gnn_in['W'], 'L1_gnn_b': _L1_gnn_in['b'], 'L2_gnn_W': _L2_gnn_in['W'], 'L2_gnn_b': _L2_gnn_in['b'], 'L3_gnn_W': _L3_gnn_in['W'], 'L3_gnn_b': _L3_gnn_in['b']}

def reference(x, adj, L0_gnn_weightr, L0_gnn_weightd, L0_gnn_bias, L1_gnn_W, L1_gnn_b, L2_gnn_W, L2_gnn_b, L3_gnn_W, L3_gnn_b):
    import jax
    import jax.numpy as jnp

    def _L0_gnn_ref(x, adj, weightr, weightd, bias):
        import jax, jax.numpy as jnp
        import numpy as np
        SIZE_U = 2048
        SIZE_V = 2048
        N = SIZE_U + SIZE_V
        C_IN = 256
        C_OUT = 256
        EDGE_P = 0.005
        LEAKY_SLOPE = 0.01

        def _xavier_uniform(key, shape):
            fan_in, fan_out = shape
            lim = float(np.sqrt(6.0 / (fan_in + fan_out)))
            return jax.random.uniform(key, shape, jnp.float32, minval=-lim, maxval=lim)
        A = adj + jnp.eye(N, dtype=adj.dtype)
        deg = A.sum(axis=1)
        dinv = jnp.where(deg > 0, jax.lax.rsqrt(deg), 0.0)
        A = A * dinv[:, None] * dinv[None, :]
        R = x[:SIZE_U] @ weightr
        D = x[SIZE_U:] @ weightd
        h = jnp.concatenate([R, D], axis=0)
        out = A @ h + bias
        return jax.nn.leaky_relu(out, negative_slope=LEAKY_SLOPE)

    def _L1_gnn_ref(x, adj, W, b):
        import jax, jax.numpy as jnp
        import numpy as np
        EPS = 1e-08
        deg = adj.sum(axis=1)
        dis = (deg + EPS) ** (-0.5)
        a_norm = dis[:, None] * adj * dis[None, :]
        h = a_norm @ x
        return h @ W.T + b

    def _L2_gnn_ref(H, adj_matrix, W, b):
        import jax, jax.numpy as jnp
        import numpy as np
        N, NIN, NOUT = (4096, 256, 256)
        n = adj_matrix.shape[0]
        A = adj_matrix + jnp.eye(n, dtype=adj_matrix.dtype)
        deg = jnp.sum(A, axis=0)
        d = deg ** (-0.5)
        d = jnp.where(jnp.isinf(d), 0.0, d)
        A = d[:, None] * A * d[None, :]
        Hm = A @ H
        out = jnp.tanh(Hm @ W.T + b)
        return out

    def _L3_gnn_ref(x, adjacency, node_degree, W, b):
        import jax, jax.numpy as jnp
        import numpy as np
        N = 8192
        D_IN = 256
        D_OUT = 256
        AVG_DEG = 32.0
        n = adjacency.shape[0]
        a_hat = adjacency + jnp.eye(n, dtype=adjacency.dtype)
        dinv = jax.lax.rsqrt(node_degree)
        a_norm = dinv * a_hat * dinv
        pooled = a_norm @ x + x
        return jax.nn.relu(pooled @ W + b)
    deg = jnp.maximum((adj != 0).astype(jnp.float32).sum(-1), 1.0)
    h = jnp.maximum(_layernorm(x, axis=-1), 0.0)
    x = x + _L0_gnn_ref(h, adj, L0_gnn_weightr, L0_gnn_weightd, L0_gnn_bias)
    h = jnp.maximum(_layernorm(x, axis=-1), 0.0)
    x = x + _L1_gnn_ref(h, adj, L1_gnn_W, L1_gnn_b)
    h = jnp.maximum(_layernorm(x, axis=-1), 0.0)
    x = x + _L2_gnn_ref(h, adj, L2_gnn_W, L2_gnn_b)
    h = jnp.maximum(_layernorm(x, axis=-1), 0.0)
    x = x + _L3_gnn_ref(h, adj, deg[..., None], L3_gnn_W, L3_gnn_b)
    return x

_drawn_inputs = setup_inputs


def setup_inputs(seed=0):
    import zlib

    import numpy as np

    out = dict(_drawn_inputs(seed))
    spreads = {'L0_gnn_bias': (0.0, 0.1), 'L2_gnn_b': (0.0, 0.1)}
    factors = {'L1_gnn_b': 8.0, 'L3_gnn_b': 8.0}
    for name, (base, spread) in spreads.items():
        noise = np.random.default_rng([zlib.crc32(name.encode()), seed]).standard_normal(out[name].shape)
        drawn = base * np.exp(spread * noise) if base else spread * noise
        out[name] = jnp.asarray(drawn.astype(out[name].dtype))
    for name, factor in factors.items():
        out[name] = (out[name] * factor).astype(out[name].dtype)
    return out
```

```python
import concourse.bass as bass
from concourse import mybir
from contextlib import ExitStack

P = 128
N = 4096
C = 256
T = N // P
KT = C // P
CHUNK = 512
CT = CHUNK // P
NCH = N // CHUNK
HALF = T // 2
STREAMED = 3
RING = 4
H_BOUND = C ** 0.5
G_SCALE = 2.0 ** 15 / H_BOUND
LN_EPS = 1e-5
LEAK = 0.01

F32 = mybir.dt.float32
F16 = mybir.dt.float16
F8 = mybir.dt.float8e4
I32 = mybir.dt.int32
ALU = mybir.AluOpType
ACT = mybir.ActivationFunctionType
AX = mybir.AxisListType


def build(nc, x_in, adj, wr, wd, b0, w1t, b1, w2t, b2, w3, b3, out):
    ctx = ExitStack()
    with ctx:
        def sb(name, shape, dt):
            return ctx.enter_context(nc.sbuf_tensor(name, shape, dt))

        def sem(name):
            return ctx.enter_context(nc.semaphore(name))

        slab_words = CHUNK // 4
        scratch = nc.dram_tensor("adj8_scratch", (NCH, P, T, slab_words), F32, kind="Internal").ap()

        g = sb("g", [P, 2, T, 2, C], F16)
        stage = g[:, 1].rearrange("p t s c -> p (t s c)").bitcast(F32) \
                       .rearrange("p (s n) -> p s n", s=4)
        ring_words = sb("ring", [P, RING, HALF * slab_words], F32)
        ring = ring_words[:, :, :].bitcast(F8).rearrange("p s (t n) -> p s t n", n=CHUNK)
        a8_words = sb("a8", [P, 2, N // 4], F32)
        a8 = a8_words[:, :, :].bitcast(F8)
        x = sb("x", [P, T, C], F32)
        pooledT = sb("pooledT", [P, 3, KT, CHUNK], F32)
        w_proj = sb("w_proj", [P, 4, KT, C], F32)
        w_in = sb("w_in", [P, 2, KT, C], F32)
        bias = sb("bias", [P, 4, C], F32)
        hn = sb("hn", [P, 2, C], F32)
        hT = sb("hT", [P, KT, 2, P], F32)
        u = sb("u", [P, CT, C], F32)
        v = sb("v", [P, CT, C], F32)
        gfull = sb("gfull", [P, CT, C], F32)
        ident = sb("ident", [P, P], F32)
        diag = sb("diag", [P, T, 2, P], F16)
        neg_ident = sb("neg_ident", [P, P], F16)
        rowsum = sb("rowsum", [P, 2, 2], F32)
        deg1 = sb("deg1", [P, T], F32)
        deg = sb("deg", [P, T], F32)
        deg_hi = sb("deg_hi", [P, T], F16)
        deg_hi32 = sb("deg_hi32", [P, T], F32)
        deg_lo32 = sb("deg_lo32", [P, T], F32)
        dinv1 = sb("dinv1", [P, T], F32)
        dinv = sb("dinv", [P, T], F32)
        out_scale = sb("out_scale", [P, 4, T], F32)
        g_scale = sb("g_scale", [P, 4, T], F32)
        wmax_part = sb("wmax_part", [P, 2], F32)
        wmax = sb("wmax", [P, 2], F32)
        stats = sb("stats", [P, CT, 6], F32)
        mv = sb("mv", [P, CT, 2], F32)
        var = sb("var", [P, T], F32)
        rstd = sb("rstd", [P, T], F32)
        ln_scale = sb("ln_scale", [P, CT], F32)
        newton_a = sb("newton_a", [P, T], F32)
        newton_b = sb("newton_b", [P, T], F32)

        bank = [ctx.enter_context(nc.psum_tensor(f"bank{k}", [P, CHUNK], F32)) for k in range(8)]

        def acc(ch):
            k = 2 * ((ch + 1) % 2)
            return bank[k], bank[k + 1]

        def acc_streamed(ch):
            return bank[2 * ch], bank[2 * ch + 1]

        def y_of(ch, q):
            return bank[4 + 2 * ((ch + 1) % 2) + q // 2][:, (q % 2) * C:(q % 2 + 1) * C]

        hT_bank, y0_bank = bank[6], bank[7]

        consts_in = sem("consts_in")
        x_first_in = sem("x_first_in")
        x_rest_in = sem("x_rest_in")
        proj_in = sem("proj_in")
        stage_in = [sem(f"stage_in{s}") for s in range(4)]
        slab_in = [sem(f"slab_in{s}") for s in range(RING)]
        ident_made = sem("ident_made")
        wmax_part_made = sem("wmax_part_made")
        wmax_made = sem("wmax_made")
        diag_added = sem("diag_added")
        a8_made = sem("a8_made")
        a8_used = sem("a8_used")
        a8_stored = [sem("a8_stored0"), sem("a8_stored1")]
        h_made = sem("h_made")
        hT_done = sem("hT_done")
        hT_copied = sem("hT_copied")
        y0_done = sem("y0_done")
        g0_made = sem("g0_made")
        first_half_used = sem("first_half_used")
        acc_done = sem("acc_done")
        pooled_made = sem("pooled_made")
        y_done = sem("y_done")
        y_read = sem("y_read")
        tanh_in = sem("tanh_in")
        tanh_done = sem("tanh_done")
        gfull_made = sem("gfull_made")
        hi_made = sem("hi_made")
        g_made = sem("g_made")
        x_done = sem("x_done")
        out_stored = sem("out_stored")
        diag_made = sem("diag_made")
        waits_past = sem("waits_past")
        dve_step = sem("dve_step")
        act_step = sem("act_step")
        pool_step = sem("pool_step")

        block = ctx.enter_context(nc.Block())

        adj_pairs = adj.rearrange("(i b p) (h n) -> i b p h n", b=2, p=P, h=2)
        x_tiles = x_in.rearrange("(t p) c -> p t c", p=P)
        out_chunks = out.rearrange("(n t p) c -> n p t c", p=P, t=CT)

        def slot_of(ch, half):
            return (2 * ch + half) % RING

        def slot_fill(layer, ch, half):
            s = slot_of(ch, half)
            first = next(m for m in range(2 * STREAMED, 2 * STREAMED + RING) if m % RING == s)
            return ((layer * NCH + ch) * 2 + half - first) // RING + 1

        def wait_past(eng, own, sem_, value):
            eng.wait_ge(sem_, value)
            if not isinstance(value, int):
                eng.sem_inc(waits_past, 1)

        @block.sync
        def _(sp):
            for k, w in enumerate((wr, wd)):
                sp.dma_start(w_in[:, k], w.rearrange("(k p) n -> p k n", p=P)).then_inc(consts_in, 16)
            for l, b in enumerate((b0, b1, b2, b3)):
                sp.dma_start(bias[:, l, :], b.rearrange("(a c) -> a c", a=1).to_broadcast([P, C])) \
                    .then_inc(consts_in, 16)
            sp.dma_start(x[:, 0:4, :], x_tiles[:, 0:4, :]).then_inc(x_first_in, 16)

            def load_pair(i, first):
                for s in range(4):
                    if not first:
                        sp.wait_ge(a8_made, i * 4 + (s - 3))
                    sp.dma_start(stage[:, s, :], adj_pairs[i, s // 2, :, s % 2, :]) \
                        .then_inc(stage_in[s], 16)

            load_pair(0, True)
            sp.dma_start(x[:, 4:T, :], x_tiles[:, 4:T, :]).then_inc(x_rest_in, 16)
            for k, w in enumerate((w1t, w2t, w3)):
                sp.dma_start(w_proj[:, k + 1], w.rearrange("(k p) n -> p k n", p=P)).then_inc(proj_in, 16)
            with nc.sync.Fori(1, T // 2) as i:
                load_pair(i, False)

            scratch_pairs = scratch.rearrange("(n b) p t w -> n b p t w", b=2)

            for b in range(2):
                sp.wait_ge(a8_stored[b], 16 * (T // 2))
            for ch in range(STREAMED, NCH):
                for half in range(2):
                    if ch >= STREAMED + 2:
                        sp.wait_ge((first_half_used, acc_done)[half], ch - STREAMED - 1)
                    sp.dma_start(ring_words[:, slot_of(ch, half), :],
                                 scratch[ch, :, half * HALF:(half + 1) * HALF, :]) \
                        .then_inc(slab_in[slot_of(ch, half)], 16)
            with nc.sync.Fori(NCH // 2, 2 * NCH) as pair:
                for b in range(2):
                    for half in range(2):
                        sp.wait_ge((first_half_used, acc_done)[half], pair * 2 + (b - STREAMED - 1))
                        sp.dma_start(ring_words[:, slot_of(b, half), :],
                                     scratch_pairs[pair % (NCH // 2), b, :, half * HALF:(half + 1) * HALF, :]) \
                            .then_inc(slab_in[slot_of(b, half)], 16)

        @block.gpsimd
        def _(pool):
            pool.memset(ident[:, :], 0.0).then_inc(pool_step, 1)
            pool.wait_ge(pool_step, 1)
            pool.affine_select(out=ident[:, :], in_=ident[:, :], compare_op=ALU.not_equal, fill=1.0,
                               base=0, pattern=[[-1, P]], channel_multiplier=1).then_inc(ident_made, 1)
            pool.wait_ge(wmax_part_made, 1)
            pool.partition_all_reduce(wmax[:, 0:1], wmax_part[:, 0:1], P,
                                      bass.bass_isa.ReduceOp.max).then_inc(wmax_made, 1)
            pool.wait_ge(ident_made, 1)

            def add_ident(i, b):
                for h in range(2):
                    pool.wait_ge(stage_in[2 * b + h], i * 16 + 16)
                rows = stage[:, 2 * b:2 * b + 2, :].rearrange("p s n -> p (s n)")
                at = rows[:, bass.ds(i * (2 * P) + b * P, P)]
                pool.tensor_tensor(at, at, ident[:, :], ALU.add).then_inc(diag_added, 1)

            def store(i, b):
                pool.wait_ge(a8_made, i * 4 + (2 * b + 2))
                pool.dma_start(scratch[:, :, i * 2 + b, :].rearrange("n p w -> p n w"),
                               a8_words[:, b, :].rearrange("p (n w) -> p n w", n=NCH)) \
                    .then_inc(a8_stored[b], 16)

            add_ident(0, 0)
            add_ident(0, 1)
            with nc.gpsimd.Fori(1, T // 2) as i:
                store(i - 1, 0)
                add_ident(i, 0)
                store(i - 1, 1)
                add_ident(i, 1)
            for b in range(2):
                store(T // 2 - 1, b)

            with nc.gpsimd.Fori(0, NCH) as ch:
                pool.wait_ge(x_done, ch + 1)
                pool.dma_start(out_chunks[ch], x[:, bass.ds(ch * CT, CT), :]).then_inc(out_stored, 16)
            pool.wait_ge(out_stored, 16 * NCH)

        @block.tensor
        def _(pe):
            def transpose_h(i):
                pe.wait_ge(h_made, i + 1)
                if i >= 1:
                    pe.wait_ge(hT_copied, i)
                for k in range(KT):
                    for b in range(2):
                        last = nc.tensor.transpose(hT_bank[:, (k * 2 + b) * P:(k * 2 + b + 1) * P],
                                                   hn[:, b, k * P:(k + 1) * P], ident[:, :])
                last.then_inc(hT_done, 1)

            def input_product(i):
                pe.wait_ge(hT_copied, i + 1)
                for b in range(2):
                    for k in range(KT):
                        last = nc.tensor.matmul(y0_bank[:, b * C:(b + 1) * C], hT[:, k, b, :],
                                                w_in[:, i // (T // 4), k, :],
                                                start=(k == 0), stop=(k == KT - 1))
                last.then_inc(y0_done, 1)

            pe.wait_ge(ident_made, 1)
            pe.wait_ge(consts_in, 16 * 6)
            transpose_h(0)
            input_product(0)
            for i in range(T // 2):
                if i + 1 < T // 2:
                    transpose_h(i + 1)
                pe.wait_ge(g0_made, i + 1)
                for b in range(2):
                    j = 2 * i + b
                    pe.wait_ge(a8_made, 2 * j + 2)
                    for s in range(2):
                        for c in range(KT):
                            for ch in range(STREAMED):
                                last = nc.tensor.matmul(
                                    acc_streamed(ch)[c][:, :], g[:, 0, j, s, c * P:(c + 1) * P],
                                    a8[:, b, ch * CHUNK:(ch + 1) * CHUNK],
                                    start=(j == 0 and s == 0), stop=(j == T - 1 and s == 1))
                    last.then_inc(a8_used, 1)
                    if b == 0 and i + 1 < T // 2:
                        input_product(i + 1)

            def pool_blocks(layer, ch, js, first, last_step, n=None):
                for j in js:
                    half = j // HALF
                    if j == 0 and n is not None:
                        pe.wait_ge(pooled_made, n * 2 - 2)
                    if layer > 0 and j % CT == 0:
                        pe.wait_ge(g_made, (layer - 1) * NCH + j // CT + 1)
                    if j % HALF == 0:
                        wait_past(pe, nc.tensor, slab_in[slot_of(ch, half)], first[half])
                    for c in range(KT):
                        for s in range(2):
                            done = nc.tensor.matmul(
                                acc(ch)[c][:, :],
                                g[:, layer % 2, j, s, c * P:(c + 1) * P],
                                ring[:, slot_of(ch, half), j % HALF, :],
                                start=(j == 0 and s == 0),
                                stop=(last_step and j == T - 1 and s == 1))
                    if j == HALF - 1:
                        done.then_inc(first_half_used, 1)
                return done

            def add_diagonal(layer, ch, parity):
                parts = [neg_ident[:, :]] if layer == 1 else None
                for q in range(CT):
                    t = ch * CT + q
                    for c in range(KT):
                        for s in range(2):
                            lhsT = g[:, layer % 2, t, s, c * P:(c + 1) * P]
                            for m in range(1 if layer == 1 else 2):
                                rhs = parts[0] if layer == 1 else diag[:, t, m, :]
                                final = s == 1 and m == (0 if layer == 1 else 1) and q == CT - 1
                                done = nc.tensor.matmul(
                                    acc(parity)[c][:, q * P:(q + 1) * P],
                                    lhsT, rhs, start=False, stop=final)
                return done

            def chunk(layer, ch, parity, n, fills, before):
                pool_blocks(layer, parity, range(0, CT), fills, False, n)
                before()
                diagonal = layer in (1, 3)
                done = pool_blocks(layer, parity, range(CT, T), fills, not diagonal)
                if diagonal:
                    done = add_diagonal(layer, ch, parity)
                done.then_inc(acc_done, 1)

            def project(parity, n, weights, pooled=None):
                src = parity if pooled is None else pooled
                pe.wait_ge(pooled_made, n * 2 + 2)
                pe.wait_ge(y_read, n - 1)
                for q in range(CT):
                    for k in range(KT):
                        done = nc.tensor.matmul(y_of(parity, q), pooledT[:, src, k, q * P:(q + 1) * P],
                                                weights[:, k, :], start=(k == 0), stop=(k == KT - 1))
                done.then_inc(y_done, 1)

            def untranspose(ch, n, pooled=None, y_free=True):
                src = ch % 2 if pooled is None else pooled
                pe.wait_ge(pooled_made, n * 2 + 2)
                if y_free:
                    pe.wait_ge(y_read, n - 1)
                for q in range(CT):
                    for k in range(KT):
                        done = nc.tensor.transpose(y_of(ch % 2, q)[:, k * P:(k + 1) * P],
                                                   pooledT[:, src, k, q * P:(q + 1) * P], ident[:, :])
                done.then_inc(y_done, 1)

            def untranspose_streamed():
                untranspose(0, 0, y_free=False)
                pe.wait_ge(pooled_made, 2 * STREAMED)
                untranspose(1, 1, y_free=False)

            def fills0(ch):
                return [16 * slot_fill(0, ch, 0), 16 * slot_fill(0, ch, 1)]

            pe.wait_ge(pooled_made, 2)
            ch = STREAMED
            pool_blocks(0, 1, range(0, CT), fills0(ch), False)
            untranspose_streamed()
            pool_blocks(0, 1, range(CT, HALF), fills0(ch), False)
            untranspose(2, 2, pooled=2)
            pool_blocks(0, 1, range(HALF, T), fills0(ch), True).then_inc(acc_done, 1)
            with nc.tensor.Fori((STREAMED + 1) // 2, NCH // 2) as pair:
                for b in range(2):
                    n = pair * 2 + b
                    fills = [(pair + (slot_fill(0, STREAMED + 1 + b, h) - (STREAMED + 1) // 2)) * 16
                             for h in range(2)]
                    chunk(0, n, b, n, fills, lambda: untranspose(1 - b, n - 1))

            pe.wait_ge(proj_in, 16 * 3)
            for layer in range(1, 4):
                if layer == 3:
                    pe.wait_ge(diag_made, 1)
                with nc.tensor.Fori(0, NCH // 2) as pair:
                    own = (pair + (NCH // 2 - 1)) // (NCH // 2) + (layer - 1)
                    for b in range(2):
                        ch = pair * 2 + b
                        n = ch + layer * NCH
                        fills = [(pair + slot_fill(layer, b, h)) * 16 for h in range(2)]
                        w = w_proj[:, own] if b == 0 else w_proj[:, layer]
                        chunk(layer, ch, b, n, fills, lambda: project(1 - b, n - 1, w))
            project(1, 4 * NCH - 1, w_proj[:, 3])

        @block.scalar
        def _(act):
            def convert(i, b, first):
                if not first:
                    act.wait_ge(a8_used, i * 2 + (b - 1))
                    act.wait_ge(a8_stored[b], i * 16)
                    act.wait_ge(g0_made, i)
                wait_past(act, nc.scalar, diag_added, i * 2 + (b + 1))
                for h in range(2):
                    nc.scalar.activation(a8[:, b, h * (N // 2):(h + 1) * (N // 2)], stage[:, 2 * b + h, :],
                                         ACT.Copy, accum_out=rowsum[:, b, h:h + 1], saturate=False) \
                        .then_inc(a8_made, 1)

            def copy_hT(i, first):
                act.wait_ge(hT_done, i + 1)
                if not first:
                    act.wait_ge(y0_done, i)
                nc.scalar.copy(hT[:, :, :, :].rearrange("p k b n -> p (k b n)"), hT_bank[:, :]) \
                    .then_inc(hT_copied, 1)

            copy_hT(0, True)
            convert(0, 0, True)
            copy_hT(1, False)
            convert(0, 1, True)
            with nc.scalar.Fori(1, T // 2 - 1) as i:
                convert(i, 0, False)
                copy_hT(i + 1, False)
                convert(i, 1, False)
            for b in range(2):
                convert(T // 2 - 1, b, False)

            act.wait_ge(a8_used, T)
            for ch in range(STREAMED):
                for c in range(KT):
                    nc.scalar.copy(pooledT[:, ch, c, :], acc_streamed(ch)[c][:, :]).then_inc(pooled_made, 1)

            def copy_pooled(parity, n):
                act.wait_ge(acc_done, n - (STREAMED - 1))
                act.wait_ge(y_done, n - 1)
                for c in range(KT):
                    nc.scalar.copy(pooledT[:, parity, c, :], acc(parity)[c][:, :]) \
                        .then_inc(pooled_made, 1)

            def g_hi(layer, ch, n):
                if layer == 3:
                    return
                if layer == 2:
                    act.wait_ge(tanh_in, ch + 1)
                    nc.scalar.activation(v[:, :, :], u[:, :, :], ACT.Tanh).then_inc(tanh_done, 1)
                act.wait_ge(gfull_made, n + 1)
                nc.scalar.activation(g[:, (layer + 1) % 2, bass.ds(ch * CT, CT), 0, :], gfull[:, :, :],
                                     ACT.Relu).then_inc(hi_made, 1)

            for ch in range(STREAMED):
                g_hi(0, ch, ch)
            copy_pooled(1, STREAMED)
            g_hi(0, STREAMED, STREAMED)
            for layer in range(4):
                with nc.scalar.Fori((STREAMED + 1) // 2 if layer == 0 else 0, NCH // 2) as pair:
                    for b in range(2):
                        ch = pair * 2 + b
                        copy_pooled(b, ch + layer * NCH)
                        g_hi(layer, ch, ch + layer * NCH)

        @block.vector
        def _(dve):
            class Steps:
                def __init__(self):
                    self.base, self.taken = 0, 0

                def after(self, ins, before_norm=False):
                    ins.then_inc(dve_step, 1)
                    self.taken += 1
                    if before_norm:
                        wait_past(dve, nc.vector, dve_step, self.base + self.taken)
                    else:
                        dve.wait_ge(dve_step, self.base + self.taken)

                def loop(self, start, stop, body, per_pass):
                    total = self.base + self.taken
                    with nc.vector.Fori(start, stop) as i:
                        self.base = (i - start) * per_pass + total
                        self.taken = 0
                        body(i)
                        assert self.taken == per_pass, (self.taken, per_pass)
                    self.base = 0
                    self.taken = total + per_pass * (stop - start)

            st = Steps()
            after = st.after
            V = nc.vector

            def rsqrt(dst, src, a, b):
                after(V.tensor_scalar(a.bitcast(I32), src.bitcast(I32), 1, None, ALU.logical_shift_right))
                after(V.tensor_scalar(dst.bitcast(I32), a.bitcast(I32), -1.0, float(0x5f3759df),
                                      ALU.mult, ALU.add))
                for _ in range(3):
                    after(V.tensor_tensor(a, dst, dst, ALU.mult))
                    after(V.scalar_tensor_tensor(b, a, -0.5, src, ALU.mult, ALU.mult))
                    after(V.scalar_tensor_tensor(dst, b, 1.5, dst, ALU.add, ALU.mult))

            RSQRT_STEPS = 11

            def norm_stats(t, n):
                for q in range(n):
                    last = V.bn_stats(stats[:, q, :], x[:, t + q, :])
                after(last, before_norm=True)
                for q in range(n):
                    last = V.bn_aggr(mv[:, q, :], stats[:, q, :])
                after(last)
                after(V.tensor_scalar(var[:, 0:n], mv[:, 0:n, 1], LN_EPS, None, ALU.add))
                rsqrt(rstd[:, 0:n], var[:, 0:n], newton_a[:, 0:n], newton_b[:, 0:n])

            NORM_STEPS = 3 + RSQRT_STEPS

            def norm_pair(i, first):
                norm_stats(i * 2, 2)
                if not first:
                    dve.wait_ge(hT_done, i)
                for b in range(2):
                    last = V.tensor_scalar(gfull[:, b, :], x[:, i * 2 + b, :], mv[:, b, 0:1],
                                           rstd[:, b:b + 1], ALU.subtract, ALU.mult)
                after(last)
                V.tensor_scalar(hn[:, :, :], gfull[:, 0:2, :], 0.0, None, ALU.max).then_inc(h_made, 1)

            def g_pair(i):
                dve.wait_ge(a8_made, i * 4 + 4)
                cols = bass.ds(i * 2, 2)
                after(V.tensor_tensor(deg1[:, cols], rowsum[:, :, 0], rowsum[:, :, 1], ALU.add))
                rsqrt(dinv1[:, cols], deg1[:, cols], newton_a[:, 0:2], newton_b[:, 0:2])
                after(V.tensor_scalar(g_scale[:, 0, cols], dinv1[:, cols], wmax[:, 1:2], None, ALU.mult))
                dve.wait_ge(y0_done, i + 1)
                for b in range(2):
                    last = V.tensor_scalar(u[:, b, :], y0_bank[:, b * C:(b + 1) * C],
                                           g_scale[:, 0, bass.ds(i * 2 + b, 1)], None, ALU.mult)
                after(last)
                pair = g[:, 0, cols]
                after(V.tensor_copy(pair[:, :, 0, :], u[:, 0:2, :]))
                V.tensor_tensor(pair[:, :, 1, :], u[:, 0:2, :], pair[:, :, 0, :], ALU.subtract) \
                    .then_inc(g0_made, 1)

            dve.wait_ge(consts_in, 16 * 6)
            V.tensor_reduce(wmax_part[:, 0:1], w_in[:, :, :, :].rearrange("p a k n -> p (a k n)"), AX.X, ALU.max,
                            apply_absolute_value=True).then_inc(wmax_part_made, 1)
            dve.wait_ge(ident_made, 1)
            for k in range(KT):
                after(V.memset(w_proj[:, 0, k, (1 - k) * P:(2 - k) * P], 0.0))
                after(V.tensor_copy(w_proj[:, 0, k, k * P:(k + 1) * P], ident[:, :]))
            after(V.tensor_scalar(neg_ident[:, :], ident[:, :], -1.0, None, ALU.mult))
            dve.wait_ge(x_first_in, 16)
            norm_pair(0, True)
            norm_pair(1, False)
            dve.wait_ge(wmax_made, 1)
            after(V.tensor_scalar(wmax[:, 0:1], wmax[:, 0:1], C * 2.0 ** -15,
                                  1e-30, ALU.mult, ALU.max))
            after(V.reciprocal(wmax[:, 1:2], wmax[:, 0:1]))
            dve.wait_ge(x_rest_in, 16)

            def pair_body(i):
                g_pair(i - 1)
                norm_pair(i + 1, False)

            G_STEPS = 1 + RSQRT_STEPS + 3
            st.loop(1, T // 2 - 1, pair_body, G_STEPS + NORM_STEPS + 1)
            g_pair(T // 2 - 2)
            g_pair(T // 2 - 1)

            after(V.tensor_scalar(deg[:, :], deg1[:, :], -1.0, 1.0, ALU.add, ALU.max))
            rsqrt(dinv[:, :], deg[:, :], newton_a[:, :], newton_b[:, :])
            V.tensor_scalar(out_scale[:, 0, :], dinv1[:, :], wmax[:, 0:1], None, ALU.mult)
            V.tensor_scalar(out_scale[:, 1, :], dinv[:, :], 1.0 / G_SCALE, None, ALU.mult)
            V.tensor_scalar(out_scale[:, 2, :], dinv1[:, :], 1.0 / G_SCALE, None, ALU.mult)
            after(V.reciprocal(newton_a[:, :], deg[:, :]))
            V.tensor_scalar(out_scale[:, 3, :], newton_a[:, :], 1.0 / G_SCALE, None, ALU.mult)
            V.tensor_scalar(g_scale[:, 1, :], dinv[:, :], G_SCALE, None, ALU.mult)
            V.tensor_scalar(g_scale[:, 2, :], dinv1[:, :], G_SCALE, None, ALU.mult)
            after(V.memset(g_scale[:, 3, :], G_SCALE))
            after(V.tensor_copy(deg_hi[:, :], deg[:, :]))
            after(V.tensor_copy(deg_hi32[:, :], deg_hi[:, :]))
            after(V.tensor_tensor(deg_lo32[:, :], deg[:, :], deg_hi32[:, :], ALU.subtract))
            def diag_body(t):
                V.tensor_scalar(diag[:, t, 0, :], ident[:, :], deg_hi32[:, bass.ds(t, 1)], None, ALU.mult)
                after(V.tensor_scalar(diag[:, t, 1, :], ident[:, :], deg_lo32[:, bass.ds(t, 1)], None, ALU.mult))
            st.loop(0, T, diag_body, 1)
            V.tensor_copy(stats[:, 0, 0:1], deg[:, 0:1]).then_inc(diag_made, 1)

            def finish(layer, ch, parity, n):
                t = ch * CT
                xs = x[:, bass.ds(t, CT), :]
                dve.wait_ge(y_done, n + 1)
                for q in range(CT):
                    last = V.scalar_tensor_tensor(u[:, q, :], y_of(parity, q), out_scale[:, layer, bass.ds(t + q, 1)],
                                                  bias[:, layer, :], ALU.mult, ALU.add)
                last.then_inc(y_read, 1)
                dve.wait_ge(y_read, n + 1)
                if layer == 0:
                    after(V.scalar_tensor_tensor(v[:, :, :], u[:, :, :], LEAK, u[:, :, :], ALU.mult, ALU.max))
                    after(V.tensor_tensor(xs, v[:, :, :], xs, ALU.add), before_norm=True)
                elif layer == 1:
                    after(V.tensor_tensor(xs, u[:, :, :], xs, ALU.add), before_norm=True)
                elif layer == 2:
                    V.tensor_copy(stats[:, 0, 0:1], u[:, CT - 1, 0:1]).then_inc(tanh_in, 1)
                    dve.wait_ge(tanh_done, ch + 1)
                    after(V.tensor_tensor(xs, v[:, :, :], xs, ALU.add), before_norm=True)
                else:
                    V.scalar_tensor_tensor(xs, u[:, :, :], 0.0, xs, ALU.max, ALU.add).then_inc(x_done, 1)
                    dve.wait_ge(x_done, ch + 1)
                    return
                norm_stats(t, CT)
                after(V.tensor_tensor(ln_scale[:, :], rstd[:, 0:CT], g_scale[:, layer + 1, bass.ds(t, CT)], ALU.mult))
                for q in range(CT):
                    last = V.tensor_scalar(gfull[:, q, :], x[:, t + q, :], mv[:, q, 0:1],
                                           ln_scale[:, q:q + 1], ALU.subtract, ALU.mult)
                last.then_inc(gfull_made, 1)
                dve.wait_ge(gfull_made, n + 1)
                dve.wait_ge(hi_made, n + 1)
                gs = g[:, (layer + 1) % 2, bass.ds(t, CT)]
                V.scalar_tensor_tensor(gs[:, :, 1, :], gfull[:, :, :], 0.0, gs[:, :, 0, :],
                                       ALU.max, ALU.subtract).then_inc(g_made, 1)
                dve.wait_ge(g_made, n + 1)

            for ch in range(STREAMED + 1):
                finish(0, ch, ch % 2, ch)
            finish_steps = [3 + NORM_STEPS, 2 + NORM_STEPS, 2 + NORM_STEPS, 0]

            def pair_of_chunks(layer, pair):
                for b in range(2):
                    ch = pair * 2 + b
                    finish(layer, ch, b, ch + layer * NCH)

            for layer in range(4):
                st.loop((STREAMED + 1) // 2 if layer == 0 else 0, NCH // 2,
                        lambda pair: pair_of_chunks(layer, pair), 2 * finish_steps[layer])


_INS = ["x", "adj", "L0_gnn_weightr", "L0_gnn_weightd", "L0_gnn_bias", "L1_gnn_W", "L1_gnn_b",
        "L2_gnn_W", "L2_gnn_b", "L3_gnn_W", "L3_gnn_b"]


def kernel(**inputs):
    import numpy as _np
    import concourse.bacc as _bacc
    from concourse import mybir as _mybir
    from concourse.bass_utils import run_bass_kernel_spmd as _run

    nc = _bacc.Bacc("TRN2", target_bir_lowering=False, num_devices=1)
    arrays, args = {}, []
    for name in _INS:
        a = _np.asarray(inputs[name])
        if name in ("L1_gnn_W", "L2_gnn_W"):
            a = a.T
        a = _np.ascontiguousarray(a)
        arrays[f"in_{name}"] = a
        args.append(nc.dram_tensor(f"in_{name}", a.shape, _mybir.dt.from_np(a.dtype), kind="ExternalInput").ap())
    out = nc.dram_tensor("out", (4096, 256), _mybir.dt.float32, kind="ExternalOutput").ap()
    build(nc, *args, out)
    r = _run(nc, [arrays], core_ids=[0])
    return r.results[0]["out"]
```

```python
import concourse.bass as bass
from concourse import mybir
from contextlib import ExitStack

P = 128
N = 4096
C = 256
T = N // P
KT = C // P
CHUNK = 512
CT = CHUNK // P
NCH = N // CHUNK
STREAMED = 3
H_BOUND = C ** 0.5
G_SCALE = 2.0 ** 15 / H_BOUND
LN_EPS = 1e-5
LEAK = 0.01

F32 = mybir.dt.float32
F16 = mybir.dt.float16
F8 = mybir.dt.float8e4
I32 = mybir.dt.int32
ALU = mybir.AluOpType
ACT = mybir.ActivationFunctionType
AX = mybir.AxisListType


def build(nc, x_in, adj, wr, wd, b0, w1t, b1, w2t, b2, w3, b3, out):
    ctx = ExitStack()
    with ctx:
        def sb(name, shape, dt):
            return ctx.enter_context(nc.sbuf_tensor(name, shape, dt))

        def sem(name):
            return ctx.enter_context(nc.semaphore(name))

        x_dram = nc.dram_tensor("x_between_layers", (N, C), F32, kind="Internal").ap()
        g_dram = nc.dram_tensor("g_next", (NCH, P, CT * 2 * C), F16, kind="Internal").ap()

        a8 = sb("a8", [P, T, N], F8)
        g = sb("g", [P, T, 2, C], F16)

        arena = sb("arena", [P, 4 * (N // 2)], F32)
        stage = arena[:, :].rearrange("p (s n) -> p s n", s=4)

        def part(first, words):
            return arena[:, first:first + words]

        CW = CT * C
        pooledT = part(0, 2 * CW).rearrange("p (b k n) -> p b k n", b=2, k=KT)
        x = part(2 * CW, 2 * CW).rearrange("p (b t c) -> p b t c", b=2, t=CT)
        u = part(4 * CW, CW).rearrange("p (t c) -> p t c", t=CT)
        gfull = part(5 * CW, CW).rearrange("p (t c) -> p t c", t=CT)
        g_out = part(6 * CW, CW).bitcast(F16).rearrange("p (t s c) -> p t s c", t=CT, s=2)
        diag = part(7 * CW, CW).bitcast(F16).rearrange("p (b t m n) -> p b t m n", b=2, t=CT, m=2)

        slots = sb("slots", [P, 6, KT, C], F32)
        y0 = slots[:, 0]
        x_pairs = slots[:, 1:3]
        w_in = slots[:, 3:5]
        hT = slots[:, 5].rearrange("p a c -> p (a c)").rearrange("p (k b n) -> p k b n", k=KT, b=2)
        w_proj = slots[:, 0:4]
        bias = slots[:, 4:6].rearrange("p s a c -> p (s a) c")

        ident = sb("ident", [P, P], F32)
        rowsum = sb("rowsum", [P, T, 2], F32)
        deg1 = sb("deg1", [P, T], F32)
        deg = sb("deg", [P, T], F32)
        deg_hi = sb("deg_hi", [P, T], F16)
        deg_hi32 = sb("deg_hi32", [P, T], F32)
        deg_lo32 = sb("deg_lo32", [P, T], F32)
        dinv1 = sb("dinv1", [P, T], F32)
        dinv = sb("dinv", [P, T], F32)
        out_scale = sb("out_scale", [P, 4, T], F32)
        g_scale = sb("g_scale", [P, 4, T], F32)
        wmax_part = sb("wmax_part", [P, 1], F32)
        wmax = sb("wmax", [P, 2], F32)
        stats = sb("stats", [P, CT, 6], F32)
        mv = sb("mv", [P, CT, 2], F32)
        radicand = sb("radicand", [P, CT], F32)
        root = sb("root", [P, CT], F32)
        y0_scale = sb("y0_scale", [P, 2], F32)
        ln_scale = sb("ln_scale", [P, CT], F32)
        newton_a = sb("newton_a", [P, T], F32)
        newton_b = sb("newton_b", [P, T], F32)

        bank = [ctx.enter_context(nc.psum_tensor(f"bank{k}", [P, CHUNK], F32)) for k in range(8)]

        def acc(ch):
            k = 2 * ((ch + 1) % 2)
            return bank[k], bank[k + 1]

        def acc_streamed(ch):
            return bank[2 * ch], bank[2 * ch + 1]

        def y_of(ch, q):
            return bank[4 + 2 * ((ch + 1) % 2) + q // 2][:, (q % 2) * C:(q % 2 + 1) * C]

        hT_bank, y0_bank = bank[6], bank[7]

        w_in_loaded = sem("w_in_loaded")
        bias_in = sem("bias_in")
        proj_in = sem("proj_in")
        x_pair_in = [sem("x_pair_in0"), sem("x_pair_in1")]
        stage_in = [sem(f"stage_in{s}") for s in range(4)]
        x_in_sb = [sem("x_in_sb0"), sem("x_in_sb1")]
        x_stored = [sem("x_stored0"), sem("x_stored1")]
        g_spilled = sem("g_spilled")
        g_in = [sem(f"g_in{k}") for k in range(NCH)]
        ident_made = sem("ident_made")
        wmax_part_made = sem("wmax_part_made")
        wmax_made = sem("wmax_made")
        diag_added = sem("diag_added")
        a8_made = sem("a8_made")
        streamed = sem("streamed")
        h_made = sem("h_made")
        hT_done = sem("hT_done")
        hT_copied = sem("hT_copied")
        y0_done = sem("y0_done")
        g0_made = sem("g0_made")
        proj_ident_made = sem("proj_ident_made")
        scales_made = sem("scales_made")
        acc_done = sem("acc_done")
        group_used = sem("group_used")
        diag_patched = sem("diag_patched")
        pooled_made = sem("pooled_made")
        y_done = sem("y_done")
        y_read = sem("y_read")
        tanh_in = sem("tanh_in")
        tanh_done = sem("tanh_done")
        gfull_made = sem("gfull_made")
        hi_made = sem("hi_made")
        g_made = sem("g_made")
        x_made = sem("x_made")
        diag_made = sem("diag_made")
        waits_past = sem("waits_past")
        dve_step = sem("dve_step")
        pool_step = sem("pool_step")

        block = ctx.enter_context(nc.Block())

        adj_pairs = adj.rearrange("(i b p) (h n) -> i b p h n", b=2, p=P, h=2)
        x_in_pairs = x_in.rearrange("(i b p) c -> i p b c", p=P, b=2)

        def chunks_of(a):
            return a.rearrange("(n t p) c -> n p t c", p=P, t=CT)

        def wait_past(eng, sem_, value):
            eng.wait_ge(sem_, value)
            if not isinstance(value, int):
                eng.sem_inc(waits_past, 1)

        @block.sync
        def _(sp):
            for k, w in enumerate((wr, wd)):
                sp.dma_start(w_in[:, k], w.rearrange("(k p) n -> p k n", p=P)).then_inc(w_in_loaded, 16)
            sp.dma_start(x_pairs[:, 0], x_in_pairs[0]).then_inc(x_pair_in[0], 16)
            sp.dma_start(x_pairs[:, 1], x_in_pairs[1]).then_inc(x_pair_in[1], 16)

            def load_pair(i, first):
                for s in range(4):
                    if not first:
                        sp.wait_ge(a8_made, i * 4 + (s - 3))
                    sp.dma_start(stage[:, s, :], adj_pairs[i, s // 2, :, s % 2, :]) \
                        .then_inc(stage_in[s], 16)

            load_pair(0, True)
            load_pair(1, False)
            with nc.sync.Fori(1, T // 4) as m:
                for b in range(2):
                    sp.wait_ge(hT_done, m * 2 + (b - 1))
                    sp.dma_start(x_pairs[:, b], x_in_pairs[m * 2 + b]).then_inc(x_pair_in[b], 16)
                    load_pair(m * 2 + b, False)

            sp.wait_ge(a8_made, 2 * T)
            for b in range(2):
                sp.dma_start(x[:, b], chunks_of(x_in)[b]).then_inc(x_in_sb[b], 16)
            sp.wait_ge(y0_done, T // 2)
            for l, b in enumerate((b0, b1, b2, b3)):
                sp.dma_start(bias[:, l, :], b.rearrange("(a c) -> a c", a=1).to_broadcast([P, C])) \
                    .then_inc(bias_in, 16)
            for k, w in enumerate((w1t, w2t, w3)):
                sp.dma_start(w_proj[:, k + 1], w.rearrange("(k p) n -> p k n", p=P)).then_inc(proj_in, 16)

            def after_chunk(layer, ch, b, src, src_ch):
                n = ch + layer * NCH
                sp.wait_ge(x_made, n + 1)
                sp.dma_start(chunks_of(x_dram if layer < 3 else out)[ch], x[:, b]).then_inc(x_stored[b], 16)
                if layer < 3:
                    sp.wait_ge(g_made, n + 1)
                    sp.dma_start(g_dram[ch], g_out.rearrange("p t s c -> p (t s c)")).then_inc(g_spilled, 16)
                if src is not None:
                    sp.wait_ge(x_stored[b], (ch - b) * 8 + (16 + layer * (NCH // 2) * 16))
                    sp.dma_start(x[:, b], chunks_of(src)[src_ch]).then_inc(x_in_sb[b], 16)

            for layer in range(4):
                src = x_in if layer == 0 else x_dram
                with nc.sync.Fori(0, NCH // 2 - 1) as pair:
                    for b in range(2):
                        after_chunk(layer, pair * 2 + b, b, src, pair * 2 + (b + 2))
                for b in range(2):
                    after_chunk(layer, NCH - 2 + b, b, x_dram if layer < 3 else None, b)
            for b in range(2):
                sp.wait_ge(x_stored[b], 16 * 4 * (NCH // 2))

        @block.gpsimd
        def _(pool):
            pool.memset(ident[:, :], 0.0).then_inc(pool_step, 1)
            pool.wait_ge(pool_step, 1)
            pool.affine_select(out=ident[:, :], in_=ident[:, :], compare_op=ALU.not_equal, fill=1.0,
                               base=0, pattern=[[-1, P]], channel_multiplier=1).then_inc(ident_made, 1)
            pool.wait_ge(wmax_part_made, 1)
            pool.partition_all_reduce(wmax[:, 0:1], wmax_part[:, 0:1], P,
                                      bass.bass_isa.ReduceOp.max).then_inc(wmax_made, 1)
            pool.wait_ge(ident_made, 1)

            def add_ident(i, b):
                for h in range(2):
                    pool.wait_ge(stage_in[2 * b + h], i * 16 + 16)
                rows = stage[:, 2 * b:2 * b + 2, :].rearrange("p s n -> p (s n)")
                at = rows[:, bass.ds(i * (2 * P) + b * P, P)]
                pool.tensor_tensor(at, at, ident[:, :], ALU.add).then_inc(diag_added, 1)

            with nc.gpsimd.Fori(0, T // 2) as i:
                for b in range(2):
                    add_ident(i, b)

            def patch_diagonal(layer, ch):
                if layer == 0 and ch < STREAMED:
                    pool.wait_ge(streamed, T)
                else:
                    pool.wait_ge(acc_done, layer * NCH + ch + 1 - STREAMED)
                for j in range(ch * CT, (ch + 1) * CT):
                    at = a8[:, j, j * P:(j + 1) * P]
                    last = pool.tensor_tensor(at, at, ident[:, :], ALU.subtract if layer == 0 else ALU.add,
                                              saturate=False)
                last.then_inc(diag_patched, 1)

            def bring_back(layer, k):
                group = g[:, k * CT:(k + 1) * CT].rearrange("p t s c -> p (t s c)")
                if k < NCH - 1:
                    pool.wait_ge(group_used, layer * (NCH - 1) + k + 1)
                    pool.wait_ge(g_spilled, 16 * (layer * NCH + k + 1))
                    pool.dma_start(group, g_dram[k]).then_inc(g_in[k], 16)
                else:
                    pool.wait_ge(acc_done, (layer + 1) * NCH - STREAMED)
                    pool.wait_ge(g_made, (layer + 1) * NCH)
                    pool.dma_start(group, g_out.rearrange("p t s c -> p (t s c)")).then_inc(g_in[k], 16)

            for layer in range(3):
                if layer < 2:
                    for ch in range(NCH - 1):
                        patch_diagonal(layer, ch)
                for k in range(NCH - 1):
                    bring_back(layer, k)
                if layer < 2:
                    patch_diagonal(layer, NCH - 1)
                bring_back(layer, NCH - 1)

        @block.tensor
        def _(pe):
            def transpose_h(i):
                pe.wait_ge(h_made, i + 1)
                if i >= 1:
                    pe.wait_ge(hT_copied, i)
                for k in range(KT):
                    for b in range(2):
                        last = nc.tensor.transpose(hT_bank[:, (k * 2 + b) * P:(k * 2 + b + 1) * P],
                                                   x_pairs[:, i % 2, b, k * P:(k + 1) * P], ident[:, :])
                last.then_inc(hT_done, 1)

            def input_product(i):
                pe.wait_ge(hT_copied, i + 1)
                for b in range(2):
                    for k in range(KT):
                        last = nc.tensor.matmul(y0_bank[:, b * C:(b + 1) * C], hT[:, k, b, :],
                                                w_in[:, i // (T // 4), k, :],
                                                start=(k == 0), stop=(k == KT - 1))
                last.then_inc(y0_done, 1)

            def pool_block(banks, ch, j, last_block=True):
                for c in range(KT):
                    for s in range(2):
                        done = nc.tensor.matmul(banks[c][:, :], g[:, j, s, c * P:(c + 1) * P],
                                                a8[:, j, ch * CHUNK:(ch + 1) * CHUNK],
                                                start=(j == 0 and s == 0),
                                                stop=(last_block and j == T - 1 and s == 1))
                return done

            pe.wait_ge(ident_made, 1)
            pe.wait_ge(w_in_loaded, 16 * 2)
            transpose_h(0)
            input_product(0)
            transpose_h(1)
            for i in range(T // 2):
                pe.wait_ge(g0_made, i + 1)
                if i + 1 < T // 2:
                    input_product(i + 1)
                for b in range(2):
                    j = 2 * i + b
                    pe.wait_ge(a8_made, 2 * j + 2)
                    for ch in range(STREAMED):
                        last = pool_block(acc_streamed(ch), ch, j)
                    last.then_inc(streamed, 1)
                    if b == 0 and i + 2 < T // 2:
                        transpose_h(i + 2)

            def pool_chunk(layer, ch, n, before, diagonal):
                if n is not None:
                    wait_past(pe, pooled_made, n * 2 - 2)
                if layer is not None and not diagonal:
                    wait_past(pe, diag_patched, (layer - 1) * NCH + (ch + 1))
                last_of_layer = ch == NCH - 1
                for j in range(T):
                    if layer is not None and j % CT == 0:
                        wait_past(pe, g_in[j // CT], layer * 16)
                    done = pool_block(acc(ch), ch, j, last_block=not diagonal)
                    if last_of_layer and j % CT == CT - 1 and j != T - 1 and not diagonal:
                        done.then_inc(group_used, 1)
                    for at, step in before:
                        if j == at:
                            step()
                if diagonal:
                    for q in range(CT):
                        for c in range(KT):
                            for s in range(2):
                                for m in range(2):
                                    done = nc.tensor.matmul(
                                        acc(ch)[c][:, q * P:(q + 1) * P],
                                        g[:, ch * CT + q, s, c * P:(c + 1) * P], diag[:, ch % 2, q, m, :],
                                        start=False, stop=(q == CT - 1 and s == 1 and m == 1))
                done.then_inc(acc_done, 1)

            def project(ch, n, weights):
                pe.wait_ge(pooled_made, n * 2 + 2)
                pe.wait_ge(y_read, n - 1)
                for q in range(CT):
                    for k in range(KT):
                        done = nc.tensor.matmul(y_of(ch, q), pooledT[:, ch % 2, k, q * P:(q + 1) * P],
                                                weights[:, k, :], start=(k == 0), stop=(k == KT - 1))
                done.then_inc(y_done, 1)

            def untranspose(ch):
                pe.wait_ge(pooled_made, ch * 2 + 2)
                if ch == 1:
                    pe.wait_ge(pooled_made, 2 * STREAMED)
                if ch >= 2:
                    pe.wait_ge(y_read, ch - 1)
                for q in range(CT):
                    for k in range(KT):
                        done = nc.tensor.transpose(y_of(ch, q)[:, k * P:(k + 1) * P],
                                                   pooledT[:, ch % 2, k, q * P:(q + 1) * P], ident[:, :])
                done.then_inc(y_done, 1)

            for ch in range(STREAMED, NCH):
                if ch == STREAMED:
                    pe.wait_ge(pooled_made, 2)
                    before = [(3, lambda: untranspose(0)), (7, lambda: untranspose(1)),
                              (15, lambda: untranspose(2))]
                    pool_chunk(None, ch, None, before, False)
                else:
                    pool_chunk(None, ch, ch, [(3, lambda: untranspose(ch - 1))], False)

            def pool_layer(layer, diagonal):
                for ch in range(NCH):
                    n = layer * NCH + ch
                    w = w_proj[:, layer - 1] if ch == 0 else w_proj[:, layer]
                    before = [(3, lambda: project(ch - 1, n - 1, w))]
                    if diagonal:
                        before.append((T - 1, lambda: pe.wait_ge(diag_made, ch + 1)))
                    pool_chunk(layer, ch, n, before, diagonal)

            pe.wait_ge(proj_in, 16 * 3)
            pe.wait_ge(proj_ident_made, 1)
            with nc.tensor.Fori(1, 3) as layer:
                pool_layer(layer, False)
            pool_layer(3, True)
            project(NCH - 1, 4 * NCH - 1, w_proj[:, 3])

        @block.scalar
        def _(act):
            def convert(j):
                act.wait_ge(diag_added, j + 1)
                for h in range(2):
                    nc.scalar.activation(a8[:, j, h * (N // 2):(h + 1) * (N // 2)],
                                         stage[:, 2 * (j % 2) + h, :], ACT.Copy,
                                         accum_out=rowsum[:, j, h:h + 1], saturate=False) \
                        .then_inc(a8_made, 1)

            def copy_hT(i):
                act.wait_ge(hT_done, i + 1)
                if i > 0:
                    act.wait_ge(y0_done, i)
                nc.scalar.activation(hT.rearrange("p k b n -> p (k b n)"), hT_bank[:, :], ACT.Relu) \
                    .then_inc(hT_copied, 1)

            copy_hT(0)
            for j in range(T):
                convert(j)
                if j % 2 == 1 and j > 1:
                    copy_hT(j // 2)

            act.wait_ge(streamed, T)
            act.wait_ge(scales_made, 1)
            for ch in range(STREAMED):
                if ch == 2:
                    act.wait_ge(y_done, 1)
                for c in range(KT):
                    nc.scalar.copy(pooledT[:, ch % 2, c, :], acc_streamed(ch)[c][:, :]).then_inc(pooled_made, 1)

            def copy_pooled(parity, n):
                act.wait_ge(acc_done, n - (STREAMED - 1))
                act.wait_ge(y_done, n - 1)
                for c in range(KT):
                    nc.scalar.copy(pooledT[:, parity, c, :], acc(parity)[c][:, :]).then_inc(pooled_made, 1)

            def g_hi(layer, n):
                if layer == 3:
                    return
                if layer == 2:
                    act.wait_ge(tanh_in, n - (2 * NCH - 1))
                    nc.scalar.activation(u[:, :, :], u[:, :, :], ACT.Tanh).then_inc(tanh_done, 1)
                act.wait_ge(gfull_made, n + 1)
                if layer > 0 or not isinstance(n, int) or n > 0:
                    act.wait_ge(g_spilled, n * 16)
                nc.scalar.activation(g_out[:, :, 0, :], gfull[:, :, :], ACT.Relu).then_inc(hi_made, 1)

            for ch in range(STREAMED + 1):
                if ch == STREAMED:
                    copy_pooled(ch % 2, ch)
                g_hi(0, ch)
            for layer in range(4):
                if 0 < layer < 3:
                    act.wait_ge(g_in[NCH - 1], 16 * layer)
                with nc.scalar.Fori((STREAMED + 1) // 2 if layer == 0 else 0, NCH // 2) as pair:
                    for b in range(2):
                        n = pair * 2 + (layer * NCH + b)
                        copy_pooled(b, n)
                        g_hi(layer, n)

        @block.vector
        def _(dve):
            class Steps:
                def __init__(self):
                    self.base, self.taken = 0, 0

                def after(self, ins, before_norm=False):
                    ins.then_inc(dve_step, 1)
                    self.taken += 1
                    if before_norm:
                        wait_past(dve, dve_step, self.base + self.taken)
                    else:
                        dve.wait_ge(dve_step, self.base + self.taken)

                def loop(self, start, stop, body, per_pass):
                    total = self.base + self.taken
                    with nc.vector.Fori(start, stop) as i:
                        self.base = (i - start) * per_pass + total
                        self.taken = 0
                        body(i)
                        assert self.taken == per_pass, (self.taken, per_pass)
                    self.base = 0
                    self.taken = total + per_pass * (stop - start)

            st = Steps()
            after = st.after
            V = nc.vector

            def rsqrt(dst, src, a, b):
                after(V.tensor_scalar(a.bitcast(I32), src.bitcast(I32), 1, None, ALU.logical_shift_right))
                after(V.tensor_scalar(dst.bitcast(I32), a.bitcast(I32), -1.0, float(0x5f3759df),
                                      ALU.mult, ALU.add))
                for _ in range(3):
                    after(V.tensor_tensor(a, dst, dst, ALU.mult))
                    after(V.scalar_tensor_tensor(b, a, -0.5, src, ALU.mult, ALU.mult))
                    after(V.scalar_tensor_tensor(dst, b, 1.5, dst, ALU.add, ALU.mult))

            RSQRT_STEPS = 11

            def norm_stats(tiles, n, var_out):
                for q in range(n):
                    last = V.bn_stats(stats[:, q, :], tiles[:, q, :])
                after(last, before_norm=True)
                for q in range(n):
                    last = V.bn_aggr(mv[:, q, :], stats[:, q, :])
                after(last)
                after(V.tensor_scalar(var_out, mv[:, 0:n, 1], LN_EPS, None, ALU.add))

            dve.wait_ge(w_in_loaded, 16 * 2)
            V.tensor_reduce(wmax_part[:, 0:1], w_in.rearrange("p a k n -> p (a k n)"), AX.X, ALU.max,
                            apply_absolute_value=True).then_inc(wmax_part_made, 1)
            dve.wait_ge(wmax_made, 1)
            after(V.tensor_scalar(wmax[:, 0:1], wmax[:, 0:1], C * 2.0 ** -15, 1e-30, ALU.mult, ALU.max))
            after(V.reciprocal(wmax[:, 1:2], wmax[:, 0:1]))

            def pair_step(i, parity, norm, weigh):
                if norm:
                    tiles = x_pairs[:, parity]
                    wait_past(dve, x_pair_in[parity], (i - parity) * 8 + 16)
                    norm_stats(tiles, 2, radicand[:, 2:4])
                if weigh:
                    cols = bass.ds((i - 2) * 2, 2)
                    dve.wait_ge(a8_made, i * 4 - 4)
                    after(V.tensor_tensor(radicand[:, 0:2], rowsum[:, cols, 0], rowsum[:, cols, 1], ALU.add))
                    V.tensor_copy(deg1[:, cols], radicand[:, 0:2])
                used = slice(0 if weigh else 2, 4 if norm else 2)
                rsqrt(root[:, used], radicand[:, used], newton_a[:, used], newton_b[:, used])
                if norm:
                    for b in range(2):
                        last = V.tensor_scalar(tiles[:, b, :], tiles[:, b, :], mv[:, b, 0:1],
                                               root[:, 2 + b:3 + b], ALU.subtract, ALU.mult)
                    last.then_inc(h_made, 1)
                if weigh:
                    V.tensor_copy(dinv1[:, cols], root[:, 0:2])
                    after(V.tensor_scalar(y0_scale[:, :], root[:, 0:2], wmax[:, 1:2], None, ALU.mult))
                    dve.wait_ge(y0_done, i - 1)
                    for b in range(2):
                        last = V.tensor_scalar(y0[:, b, :], y0_bank[:, b * C:(b + 1) * C],
                                               y0_scale[:, b:b + 1], None, ALU.mult)
                    after(last)
                    pair = g[:, cols]
                    after(V.tensor_copy(pair[:, :, 0, :], y0[:, :, :]))
                    V.tensor_tensor(pair[:, :, 1, :], y0[:, :, :], pair[:, :, 0, :], ALU.subtract) \
                        .then_inc(g0_made, 1)
                    dve.wait_ge(g0_made, i - 1)

            pair_step(0, 0, True, False)
            dve.wait_ge(h_made, 1)
            pair_step(1, 1, True, False)
            dve.wait_ge(h_made, 2)
            st.loop(1, T // 4, lambda m: [pair_step(m * 2 + b, b, True, True) for b in range(2)],
                    2 * (3 + 1 + RSQRT_STEPS + 3))
            for i in (T // 2, T // 2 + 1):
                pair_step(i, i % 2, False, True)

            after(V.tensor_scalar(deg[:, :], deg1[:, :], -1.0, 1.0, ALU.add, ALU.max))
            V.tensor_scalar(out_scale[:, 0, :], dinv1[:, :], wmax[:, 0:1], None, ALU.mult) \
                .then_inc(scales_made, 1)
            rsqrt(dinv[:, :], deg[:, :], newton_a[:, :], newton_b[:, :])
            V.tensor_scalar(out_scale[:, 1, :], dinv[:, :], 1.0 / G_SCALE, None, ALU.mult)
            V.tensor_scalar(out_scale[:, 2, :], dinv1[:, :], 1.0 / G_SCALE, None, ALU.mult)
            after(V.reciprocal(newton_a[:, :], deg[:, :]))
            V.tensor_scalar(out_scale[:, 3, :], newton_a[:, :], 1.0 / G_SCALE, None, ALU.mult)
            V.tensor_scalar(g_scale[:, 1, :], dinv[:, :], G_SCALE, None, ALU.mult)
            V.tensor_scalar(g_scale[:, 2, :], dinv1[:, :], G_SCALE, None, ALU.mult)
            V.memset(g_scale[:, 3, :], G_SCALE)
            after(V.tensor_copy(deg_hi[:, :], deg[:, :]))
            after(V.tensor_copy(deg_hi32[:, :], deg_hi[:, :]))
            after(V.tensor_tensor(deg_lo32[:, :], deg[:, :], deg_hi32[:, :], ALU.subtract))
            after(V.memset(w_proj[:, 0, :, :], 0.0))
            for k in range(KT):
                last = V.tensor_copy(w_proj[:, 0, k, k * P:(k + 1) * P], ident[:, :])
            last.then_inc(proj_ident_made, 1)
            dve.wait_ge(bias_in, 16 * 4)

            def make_diag(ch, parity):
                for q in range(CT):
                    t = ch * CT + q
                    V.tensor_scalar(diag[:, parity, q, 0, :], ident[:, :], deg_hi32[:, bass.ds(t, 1)], None, ALU.mult)
                    last = V.tensor_scalar(diag[:, parity, q, 1, :], ident[:, :], deg_lo32[:, bass.ds(t, 1)],
                                           None, ALU.mult)
                last.then_inc(diag_made, 1)

            def finish(layer, ch, parity):
                n = ch + layer * NCH
                t = ch * CT
                xs = x[:, parity]
                dve.wait_ge(y_done, n + 1)
                for q in range(CT):
                    last = V.scalar_tensor_tensor(u[:, q, :], y_of(parity, q), out_scale[:, layer, bass.ds(t + q, 1)],
                                                  bias[:, layer, :], ALU.mult, ALU.add)
                last.then_inc(y_read, 1)
                dve.wait_ge(y_read, n + 1)
                if layer == 0:
                    after(V.scalar_tensor_tensor(u[:, :, :], u[:, :, :], LEAK, u[:, :, :], ALU.mult, ALU.max))
                elif layer == 2:
                    V.tensor_copy(stats[:, 0, 0:1], u[:, CT - 1, 0:1]).then_inc(tanh_in, 1)
                    dve.wait_ge(tanh_done, ch + 1)
                dve.wait_ge(x_in_sb[parity], (n - parity) * 8 + 16)
                if layer == 3:
                    V.scalar_tensor_tensor(xs, u[:, :, :], 0.0, xs, ALU.max, ALU.add).then_inc(x_made, 1)
                    dve.wait_ge(x_made, n + 1)
                    return
                V.tensor_tensor(xs, u[:, :, :], xs, ALU.add).then_inc(x_made, 1)
                wait_past(dve, x_made, n + 1)
                norm_stats(xs, CT, radicand[:, 0:CT])
                rsqrt(root[:, 0:CT], radicand[:, 0:CT], newton_a[:, 0:CT], newton_b[:, 0:CT])
                after(V.tensor_tensor(ln_scale[:, :], root[:, 0:CT], g_scale[:, layer + 1, bass.ds(t, CT)], ALU.mult))
                for q in range(CT):
                    last = V.tensor_scalar(gfull[:, q, :], xs[:, q, :], mv[:, q, 0:1],
                                           ln_scale[:, q:q + 1], ALU.subtract, ALU.mult)
                last.then_inc(gfull_made, 1)
                dve.wait_ge(gfull_made, n + 1)
                dve.wait_ge(hi_made, n + 1)
                V.scalar_tensor_tensor(g_out[:, :, 1, :], gfull[:, :, :], 0.0, g_out[:, :, 0, :],
                                       ALU.max, ALU.subtract).then_inc(g_made, 1)
                dve.wait_ge(g_made, n + 1)

            for ch in range(STREAMED + 1):
                finish(0, ch, ch % 2)
            norm_steps = 3 + RSQRT_STEPS + 1
            finish_steps = [1 + norm_steps, norm_steps, norm_steps, 0]

            for layer in range(4):
                def pair_of_chunks(pair):
                    for b in range(2):
                        ch = pair * 2 + b
                        if layer == 3:
                            dve.wait_ge(acc_done, ch + (3 * NCH + 1 - STREAMED))
                        finish(layer, ch, b)
                        if layer == 3:
                            make_diag_ahead(ch, b)

                def make_diag_ahead(ch, b):
                    make_diag(ch + 2, b)

                if layer < 3:
                    st.loop((STREAMED + 1) // 2 if layer == 0 else 0, NCH // 2, pair_of_chunks,
                            2 * finish_steps[layer])
                else:
                    for b in range(2):
                        make_diag(b, b)
                    st.loop(0, NCH // 2 - 1, pair_of_chunks, 0)
                    for b in range(2):
                        finish(3, NCH - 2 + b, b)


_INS = ["x", "adj", "L0_gnn_weightr", "L0_gnn_weightd", "L0_gnn_bias", "L1_gnn_W", "L1_gnn_b",
        "L2_gnn_W", "L2_gnn_b", "L3_gnn_W", "L3_gnn_b"]


def kernel(**inputs):
    import numpy as _np
    import concourse.bacc as _bacc
    from concourse import mybir as _mybir
    from concourse.bass_utils import run_bass_kernel_spmd as _run

    nc = _bacc.Bacc("TRN2", target_bir_lowering=False, num_devices=1)
    arrays, args = {}, []
    for name in _INS:
        a = _np.asarray(inputs[name])
        if name in ("L1_gnn_W", "L2_gnn_W"):
            a = a.T
        a = _np.ascontiguousarray(a)
        arrays[f"in_{name}"] = a
        args.append(nc.dram_tensor(f"in_{name}", a.shape, _mybir.dt.from_np(a.dtype), kind="ExternalInput").ap())
    out = nc.dram_tensor("out", (4096, 256), _mybir.dt.float32, kind="ExternalOutput").ap()
    build(nc, *args, out)
    r = _run(nc, [arrays], core_ids=[0])
    return r.results[0]["out"]
```

```python
import concourse.bass as bass
from concourse import mybir
from contextlib import ExitStack

P = 128
N = 4096
C = 256
T = N // P
KT = C // P
CHUNK = 512
CT = CHUNK // P
NCH = N // CHUNK
STREAMED = 3
STAGES = 3
BURST = 7
LENGTHS = (8, 10, 12, 14, 14, 14, 20, 21, 28, 28)
H_BOUND = C ** 0.5
G_SCALE = 2.0 ** 15 / H_BOUND
H_SCALE = 2.0 ** 10
LN_EPS = 1e-5
LEAK = 0.01

F32 = mybir.dt.float32
F16 = mybir.dt.float16
F8 = mybir.dt.float8e4
I32 = mybir.dt.int32
ALU = mybir.AluOpType
ACT = mybir.ActivationFunctionType
AX = mybir.AxisListType


def plan_partials():
    halves = [(ch, 0) for ch in range(STREAMED, NCH)] + [(ch, 1) for ch in reversed(range(STREAMED, NCH))]
    units = [(ch, c, n) for (ch, c), n in zip(halves[-len(LENGTHS):], LENGTHS)]
    bursts, u, at = [], 0, 0
    for j in range(T):
        there = 2 * (j // 2) + 2
        steps = []
        while len(steps) < BURST and u < len(units) and at < min(units[u][2], there):
            steps.append((u, at))
            at += 1
        if u < len(units) and at == units[u][2]:
            u, at = u + 1, 0
        bursts.append(steps)
    assert u == len(units)
    return units, bursts


def build(nc, x_in, adj, wr, wd, b0, w1t, b1, w2t, b2, w3, b3, out):
    ctx = ExitStack()
    with ctx:
        def sb(name, shape, dt):
            return ctx.enter_context(nc.sbuf_tensor(name, shape, dt))

        def sem(name):
            return ctx.enter_context(nc.semaphore(name))

        x_dram = nc.dram_tensor("x_between_layers", (N, C), F32, kind="Internal").ap()
        g_dram = nc.dram_tensor("g_next", (NCH, P, CT * 2 * C), F16, kind="Internal").ap()

        units, bursts = plan_partials()
        first_left = {(ch, c): n for ch, c, n in units}
        partial_dram = nc.dram_tensor("partial_sums", (len(units), P, CHUNK), F32, kind="Internal").ap()

        a8 = sb("a8", [P, T, N], F8)
        g = sb("g", [P, T, 2, C], F16)

        arena = sb("arena", [P, 4 * (N // 2)], F32)
        stage = arena[:, 0:STAGES * (N // 2)].rearrange("p (s n) -> p s n", s=STAGES)

        def part(first, words):
            return arena[:, first:first + words]

        CW = CT * C
        pooledT = part(0, 2 * CW).rearrange("p (b k n) -> p b k n", b=2, k=KT)
        pooled_parts = part(0, 2 * CW).bitcast(F16).rearrange("p (b s k n) -> p b s k n", b=2, s=2, k=KT)
        x = part(2 * CW, 2 * CW).rearrange("p (b t c) -> p b t c", b=2, t=CT)
        update = part(4 * CW, CW).rearrange("p (t c) -> p t c", t=CT)
        gfull = part(5 * CW, CW).rearrange("p (t c) -> p t c", t=CT)
        g_out = part(6 * CW, CW).bitcast(F16).rearrange("p (t s c) -> p t s c", t=CT, s=2)
        w_raw = part(4 * CW, 3 * KT * C).rearrange("p (l k n) -> p l k n", l=3, k=KT)
        partial_out = part(6 * CW, CW).rearrange("p (b n) -> p b n", b=2)
        partial_in = part(7 * CW, CW).rearrange("p (k n) -> p k n", k=KT)
        w_in_raw = part(7 * CW, 2 * KT * C).rearrange("p (w k n) -> p w k n", w=2, k=KT)
        diag = part(7 * CW, CW // 2).bitcast(F16).rearrange("p (b t n) -> p b t n", b=2, t=CT)

        odd_diag = part(7 * CW + CW // 2, CT * P).rearrange("p (t n) -> p t n", t=CT)

        slots = sb("slots", [P, 6, KT, C], F32)
        y0 = slots[:, 0]
        x_pairs = slots[:, 1:3]
        w_in = slots[:, 3:5].rearrange("p w k n -> p (w k n)").bitcast(F16) \
            .rearrange("p (w s k n) -> p w s k n", w=2, s=2, k=KT)
        hT = slots[:, 5].rearrange("p a c -> p (a c)").bitcast(F16) \
            .rearrange("p (s k b n) -> p s k b n", s=2, k=KT, b=2)
        w_proj = slots[:, 0:4].rearrange("p l k n -> p (l k n)").bitcast(F16) \
            .rearrange("p (l s k n) -> p l s k n", l=4, s=2, k=KT)
        bias = slots[:, 4:6].rearrange("p s a c -> p (s a) c")

        ident = sb("ident", [P, P], F32)
        rowsum = sb("rowsum", [P, T, 2], F32)
        deg1 = sb("deg1", [P, T], F32)
        deg = sb("deg", [P, T], F32)
        deg_bits = sb("deg_bits", [P, T], I32)
        deg_odd = sb("deg_odd", [P, T], F32)
        deg_even = sb("deg_even", [P, T], F32)
        dinv1 = sb("dinv1", [P, T], F32)
        dinv = sb("dinv", [P, T], F32)
        out_scale = sb("out_scale", [P, 4, T], F32)
        g_scale = sb("g_scale", [P, 4, T], F32)
        wmax_part = sb("wmax_part", [P, 1], F32)
        wmax = sb("wmax", [P, 2], F32)
        maxes_part = sb("maxes_part", [P, 4], F32)
        maxes = sb("maxes", [P, 4], F32)
        w_unit = sb("w_unit", [P, 2, 3], F32)
        pooled_unit = sb("pooled_unit", [P, 2], F32)
        stats = sb("stats", [P, CT, 6], F32)
        mv = sb("mv", [P, CT, 2], F32)
        radicand = sb("radicand", [P, CT], F32)
        root = sb("root", [P, CT], F32)
        y0_scale = sb("y0_scale", [P, 2], F32)
        ln_scale = sb("ln_scale", [P, CT], F32)
        ln_bias = sb("ln_bias", [P, CT], F32)
        newton_a = sb("newton_a", [P, T], F32)
        newton_b = sb("newton_b", [P, T], F32)

        bank = [ctx.enter_context(nc.psum_tensor(f"bank{k}", [P, CHUNK], F32)) for k in range(8)]

        def acc(ch):
            k = 2 * ((ch + 1) % 2)
            return bank[k], bank[k + 1]

        def acc_streamed(ch):
            return bank[2 * ch], bank[2 * ch + 1]

        def y_of(ch, q):
            return bank[4 + 2 * ((ch + 1) % 2) + q // 2][:, (q % 2) * C:(q % 2 + 1) * C]

        partial_bank, input_bank = bank[6], bank[7]

        w_in_loaded = sem("w_in_loaded")
        bias_in = sem("bias_in")
        proj_in = sem("proj_in")
        x_pair_in = [sem("x_pair_in0"), sem("x_pair_in1")]
        stage_in = [sem(f"stage_in{s}") for s in range(STAGES)]
        partial_copied = sem("partial_copied")
        partial_stored = [sem("partial_stored0"), sem("partial_stored1")]
        partial_loaded = sem("partial_loaded")
        partial_added = sem("partial_added")
        partial_summed = sem("partial_summed")
        x_in_sb = [sem("x_in_sb0"), sem("x_in_sb1")]
        x_stored = [sem("x_stored0"), sem("x_stored1")]
        g_spilled = sem("g_spilled")
        g_in = [sem(f"g_in{k}") for k in range(NCH)]
        ident_made = sem("ident_made")
        wmax_part_made = sem("wmax_part_made")
        wmax_made = sem("wmax_made")
        diag_added = sem("diag_added")
        a8_made = sem("a8_made")
        streamed = sem("streamed")
        h_made = sem("h_made")
        hT_done = sem("hT_done")
        hT_copied = sem("hT_copied")
        hT_low = sem("hT_low")
        w_in_made = sem("w_in_made")
        y0_done = sem("y0_done")
        g0_made = sem("g0_made")
        maxes_part_made = sem("maxes_part_made")
        maxes_made = sem("maxes_made")
        pooled_unit_made = sem("pooled_unit_made")
        w_proj_made = sem("w_proj_made")
        acc_done = sem("acc_done")
        group_used = sem("group_used")
        diag_patched = sem("diag_patched")
        pooled_made = sem("pooled_made")
        pooled_hi = sem("pooled_hi")
        pooled_lo = sem("pooled_lo")
        last_y_done = sem("last_y_done")
        last_scaled = sem("last_scaled")
        last_x_made = sem("last_x_made")
        y_done = sem("y_done")
        y_read = sem("y_read")
        tanh_in = sem("tanh_in")
        tanh_done = sem("tanh_done")
        gfull_made = sem("gfull_made")
        ln_made = sem("ln_made")
        hi_made = sem("hi_made")
        g_made = sem("g_made")
        x_made = sem("x_made")
        odd_made = sem("odd_made")
        odd_diag_made = sem("odd_diag_made")
        diag_made = sem("diag_made")
        waits_past = sem("waits_past")
        dve_step = sem("dve_step")
        pool_step = sem("pool_step")

        block = ctx.enter_context(nc.Block())

        x_in_pairs = x_in.rearrange("(i b p) c -> i p b c", p=P, b=2)

        def chunks_of(a):
            return a.rearrange("(n t p) c -> n p t c", p=P, t=CT)

        def partials_up_to(ch):
            return sum(1 for uch, _, _ in units if uch <= ch)

        copied_behind = {j: [] for j in range(T)}
        for j, steps in enumerate(bursts):
            for u, at in steps:
                if at == units[u][2] - 1:
                    copied_behind[min(j + 3, T - 1)].append(u)

        def buffer_of(ch):
            return ch % 2 if ch < NCH - 1 else 0

        def wait_past(eng, sem_, value):
            eng.wait_ge(sem_, value)
            if not isinstance(value, int):
                eng.sem_inc(waits_past, 1)

        @block.sync
        def _(sp):
            sp.dma_start(x_pairs[:, 0], x_in_pairs[0]).then_inc(x_pair_in[0], 16)

            def load_blocks(m, blocks, first):
                for k in range(2 * blocks):
                    if not (first and k < STAGES):
                        sp.wait_ge(a8_made, m * 6 + (k + 1 - STAGES))
                    sp.dma_start(stage[:, k % STAGES, :],
                                 adj[bass.ds((m * 3 + k // 2) * P, P), (k % 2) * (N // 2):(k % 2 + 1) * (N // 2)]) \
                        .then_inc(stage_in[k % STAGES], 16)
                    if first and k == 0:
                        for i, w in enumerate((wr, wd)):
                            sp.dma_start(w_in_raw[:, i], w.rearrange("(k p) n -> p k n", p=P)).then_inc(w_in_loaded, 16)
                    if first and k == 1:
                        sp.dma_start(x_pairs[:, 1], x_in_pairs[1]).then_inc(x_pair_in[1], 16)

            load_blocks(0, 3, True)
            with nc.sync.Fori(1, T // 3) as m:
                load_blocks(m, 3, False)
            load_blocks(T // 3, T % 3, False)

            sp.wait_ge(a8_made, 2 * T)
            for k, w in enumerate((w1t, w2t, w3)):
                sp.dma_start(w_raw[:, k], w.rearrange("(k p) n -> p k n", p=P)).then_inc(proj_in, 16)
            for b in range(2):
                sp.dma_start(x[:, b], chunks_of(x_in)[b]).then_inc(x_in_sb[b], 16)
            sp.wait_ge(y0_done, T // 2)
            for l, b in enumerate((b0, b1, b2, b3)):
                sp.dma_start(bias[:, l, :], b.rearrange("(a c) -> a c", a=1).to_broadcast([P, C])) \
                    .then_inc(bias_in, 16)

            def after_chunk(layer, ch, b, src, src_ch):
                n = ch + layer * NCH
                sp.wait_ge(x_made, n + 1)
                sp.dma_start(chunks_of(x_dram if layer < 3 else out)[ch], x[:, b]).then_inc(x_stored[b], 16)
                if layer < 3:
                    sp.wait_ge(g_made, n + 1)
                    g_flat = g_out.rearrange("p t s c -> p (t s c)")
                    if isinstance(ch, int) and ch == NCH - 1:
                        sp.wait_ge(acc_done, (layer + 1) * NCH - STREAMED)
                        sp.dma_start(g[:, ch * CT:].rearrange("p t s c -> p (t s c)"), g_flat).then_inc(g_in[ch], 16)
                    else:
                        sp.dma_start(g_dram[ch], g_flat).then_inc(g_spilled, 16)
                if src is not None:
                    sp.wait_ge(x_stored[b], (ch - b) * 8 + (16 + layer * (NCH // 2) * 16))
                    sp.dma_start(x[:, b], chunks_of(src)[src_ch]).then_inc(x_in_sb[b], 16)

            for ch in range(NCH):
                after_chunk(0, ch, ch % 2, x_in if ch < NCH - 2 else x_dram, (ch + 2) % NCH)
            for layer in range(1, 4):
                src = x_dram
                with nc.sync.Fori(0, NCH // 2 - 1) as pair:
                    for b in range(2):
                        after_chunk(layer, pair * 2 + b, b, src, pair * 2 + (b + 2))
                for b in range(2 if layer < 3 else 1):
                    after_chunk(layer, NCH - 2 + b, b, x_dram if layer < 3 else None, b)
            for q in range(CT):
                sp.wait_ge(last_x_made, q + 1)
                sp.dma_start(chunks_of(out)[NCH - 1, :, q, :], x[:, 1, q, :]).then_inc(x_stored[1], 16)
            sp.wait_ge(x_stored[0], 16 * 4 * (NCH // 2))
            sp.wait_ge(x_stored[1], 16 * (4 * (NCH // 2) + CT - 1))

        @block.gpsimd
        def _(pool):
            pool.memset(ident[:, :], 0.0).then_inc(pool_step, 1)
            pool.wait_ge(pool_step, 1)
            pool.affine_select(out=ident[:, :], in_=ident[:, :], compare_op=ALU.not_equal, fill=1.0,
                               base=0, pattern=[[-1, P]], channel_multiplier=1).then_inc(ident_made, 1)
            pool.wait_ge(wmax_part_made, 1)
            pool.partition_all_reduce(wmax[:, 0:1], wmax_part[:, 0:1], P,
                                      bass.bass_isa.ReduceOp.max).then_inc(wmax_made, 1)
            pool.wait_ge(ident_made, 1)

            for j in range(T):
                pool.wait_ge(a8_made, 2 * j + 2)
                at = a8[:, j, j * P:(j + 1) * P]
                pool.tensor_tensor(at, at, ident[:, :], ALU.add, saturate=False).then_inc(diag_added, 1)
                if j == T - 1:
                    pool.wait_ge(maxes_part_made, 2)
                    pool.partition_all_reduce(maxes[:, :], maxes_part[:, :], P, bass.bass_isa.ReduceOp.max) \
                        .then_inc(maxes_made, 1)
                for u in copied_behind[j]:
                    pool.wait_ge(partial_copied, u + 1)
                    pool.dma_start(partial_dram[u], partial_out[:, u % 2, :]).then_inc(partial_stored[u % 2], 16)

            def load_partials(ch):
                for u, (uch, c, _) in enumerate(units):
                    if uch == ch:
                        pool.wait_ge(partial_stored[u % 2], 16 * (u // 2 + 1))
                        pool.dma_start(partial_in[:, c, :], partial_dram[u]).then_inc(partial_loaded, 16)

            def add_partials(ch):
                pool.wait_ge(partial_loaded, 16 * partials_up_to(ch))
                pool.wait_ge(pooled_made, 2 * (ch + 1))
                for c in range(KT):
                    if (ch, c) in first_left:
                        at = pooledT[:, buffer_of(ch), c, :]
                        pool.tensor_tensor(at, at, partial_in[:, c, :], ALU.add).then_inc(partial_added, 1)
                if ch + 1 < NCH:
                    pool.wait_ge(partial_added, partials_up_to(ch))
                    load_partials(ch + 1)

            def patch_diagonal(layer, ch):
                if layer == 0 and ch < STREAMED:
                    pool.wait_ge(streamed, T)
                else:
                    pool.wait_ge(acc_done, layer * NCH + ch + 1 - STREAMED)
                if layer == 2:
                    pool.tensor_tensor(odd_diag[:, :, :], ident.rearrange("p (a n) -> p a n", a=1).to_broadcast([P, CT, P]),
                                       deg_odd[:, ch * CT:(ch + 1) * CT].rearrange("p (t a) -> p t a", a=1)
                                       .to_broadcast([P, CT, P]), ALU.mult).then_inc(odd_diag_made, 1)
                    pool.wait_ge(odd_diag_made, ch + 1)
                for q in range(CT):
                    at = a8[:, ch * CT + q, (ch * CT + q) * P:(ch * CT + q + 1) * P]
                    last = pool.tensor_tensor(at, at, odd_diag[:, q, :] if layer == 2 else ident[:, :],
                                              ALU.subtract if layer == 0 else ALU.add, saturate=False)
                    if layer == 2 and q == CT - 1:
                        last.then_inc(diag_patched, 1)
                        pool.wait_ge(diag_patched, 2 * NCH + ch + 1)
                        return
                last.then_inc(diag_patched, 1)

            def bring_back(layer, k):
                group = g[:, k * CT:(k + 1) * CT].rearrange("p t s c -> p (t s c)")
                pool.wait_ge(group_used, layer * (NCH - 1) + k + 1)
                pool.wait_ge(g_spilled, 16 * (layer * (NCH - 1) + k + 1))
                pool.dma_start(group, g_dram[k]).then_inc(g_in[k], 16)

            load_partials(STREAMED)
            pool.wait_ge(odd_made, 1)
            for layer in range(3):
                for ch in range(NCH - 1):
                    if layer == 0 and ch >= STREAMED:
                        add_partials(ch)
                    patch_diagonal(layer, ch)
                for k in range(NCH - 1):
                    if layer == 0 and k == NCH - 3:
                        add_partials(NCH - 1)
                    bring_back(layer, k)
                patch_diagonal(layer, NCH - 1)

        @block.tensor
        def _(pe):
            def transpose_h(i):
                pe.wait_ge(h_made, i + 1)
                for k in range(KT):
                    for b in range(2):
                        last = nc.tensor.transpose(input_bank[:, (k * 2 + b) * P:(k * 2 + b + 1) * P],
                                                   x_pairs[:, i % 2, b, k * P:(k + 1) * P], ident[:, :])
                last.then_inc(hT_done, 1)

            def input_product(i):
                pe.wait_ge(hT_low, i + 1)
                for b in range(2):
                    for k in range(KT):
                        for h, w in ((0, 0), (0, 1), (1, 0)):
                            last = nc.tensor.matmul(input_bank[:, b * C:(b + 1) * C], hT[:, h, k, b, :],
                                                    w_in[:, i // (T // 4), w, k, :],
                                                    start=(k == 0 and h + w == 0), stop=(k == KT - 1 and h == 1))
                last.then_inc(y0_done, 1)

            def pool_half(bank_, ch, c, j, first, last):
                for s in range(2):
                    done = nc.tensor.matmul(bank_[:, :], g[:, j, s, c * P:(c + 1) * P],
                                            a8[:, j, ch * CHUNK:(ch + 1) * CHUNK],
                                            start=(first and s == 0), stop=(last and s == 1))
                return done

            def pool_block(banks, ch, j, last_block=True):
                for c in range(KT):
                    done = pool_half(banks[c], ch, c, j, j == 0, last_block and j == T - 1)
                return done

            def partial_burst(behind, steps):
                for u, j in steps:
                    ch, c, n = units[u]
                    if j == behind + 1:
                        pe.wait_ge(diag_added, j + 1)
                    if j == 0 and u > 0:
                        pe.wait_ge(partial_copied, u)
                    done = pool_half(partial_bank, ch, c, j, j == 0, j == n - 1)
                    if j == n - 1:
                        done.then_inc(partial_summed, 1)

            pe.wait_ge(ident_made, 1)
            transpose_h(0)
            pe.wait_ge(w_in_made, 1)
            input_product(0)
            for i in range(T // 2):
                pe.wait_ge(g0_made, i + 1)
                if i + 1 < T // 2:
                    transpose_h(i + 1)
                for b in range(2):
                    j = 2 * i + b
                    pe.wait_ge(diag_added, j + 1)
                    for ch in range(STREAMED):
                        last = pool_block(acc_streamed(ch), ch, j)
                    last.then_inc(streamed, 1)
                    partial_burst(j, bursts[j])
                    if b == 0 and i + 1 < T // 2:
                        input_product(i + 1)

            def early(ch):
                return min(min(first_left.get((ch, c), 0) for c in range(KT)) + 10, T - 1)

            def pool_chunk(layer, ch, before, diagonal):
                if layer is not None:
                    wait_past(pe, diag_patched, (layer - 1) * NCH + (ch + 1))
                last_of_layer = ch == NCH - 1
                done, groups = None, 0
                for j in range(T):
                    if layer is not None and j % CT == 0:
                        wait_past(pe, g_in[j // CT], layer * 16)
                    if layer is None:
                        for c in range(KT):
                            first = first_left.get((ch, c), 0)
                            if j >= first:
                                done = pool_half(acc(ch)[c], ch, c, j, j == first, j == T - 1)
                    else:
                        done = pool_block(acc(ch), ch, j, last_block=not diagonal)
                    passed = (j + 1) // CT
                    if last_of_layer and done is not None and groups < passed < NCH and not diagonal:
                        done.then_inc(group_used, passed - groups)
                        groups = passed
                    for at, step in before:
                        if j == at:
                            step()
                if diagonal:
                    for q in range(CT):
                        for c in range(KT):
                            for s in range(2):
                                done = nc.tensor.matmul(
                                    acc(ch)[c][:, q * P:(q + 1) * P],
                                    g[:, ch * CT + q, s, c * P:(c + 1) * P], diag[:, ch % 2, q, :],
                                    start=False, stop=(q == CT - 1 and s == 1))
                done.then_inc(acc_done, 1)

            def project_tile(y, q, k, parity, weights):
                for p, w in ((0, 0), (0, 1), (1, 0)):
                    done = nc.tensor.matmul(y, pooled_parts[:, parity, p, k, q * P:(q + 1) * P], weights[:, w, k, :],
                                            start=(k == 0 and p + w == 0), stop=(k == KT - 1 and p == 1))
                return done

            def project(ch, n, weights):
                pe.wait_ge(pooled_lo, n * 2 - (2 * NCH - 4))
                pe.wait_ge(y_read, n - 1)
                for q in range(CT):
                    for k in range(KT):
                        done = project_tile(y_of(ch, q), q, k, ch % 2, weights)
                done.then_inc(y_done, 1)

            def untranspose(ch):
                pe.wait_ge(pooled_made, ch * 2 + 2)
                if ch >= STREAMED:
                    pe.wait_ge(partial_added, partials_up_to(ch))
                if ch == 0:
                    pe.wait_ge(partial_copied, len(units))
                if ch == 1:
                    pe.wait_ge(pooled_made, 2 * STREAMED)
                if ch >= 2:
                    pe.wait_ge(y_read, ch - 1)
                for q in range(CT):
                    for k in range(KT):
                        done = nc.tensor.transpose(y_of(ch, q)[:, k * P:(k + 1) * P],
                                                   pooledT[:, buffer_of(ch), k, q * P:(q + 1) * P], ident[:, :])
                done.then_inc(y_done, 1)

            for ch in range(STREAMED, NCH):
                if ch == STREAMED:
                    pe.wait_ge(pooled_made, 2)
                    before = [(2, lambda: untranspose(0)), (8, lambda: untranspose(1)),
                              (16, lambda: untranspose(2))]
                    pool_chunk(None, ch, before, False)
                else:
                    pool_chunk(None, ch, [(early(ch), lambda: untranspose(ch - 1))], False)

            def pool_layer(layer, diagonal):
                for ch in range(NCH):
                    n = layer * NCH + ch
                    w = w_proj[:, layer - 1] if ch == 0 else w_proj[:, layer]
                    before = [(3 if ch > 0 else 6, lambda: project(ch - 1, n - 1, w))]
                    if diagonal:
                        before.append((T - 1, lambda: pe.wait_ge(diag_made, ch + 1)))
                    pool_chunk(layer, ch, before, diagonal)

            pe.wait_ge(w_proj_made, 1)
            with nc.tensor.Fori(1, 3) as layer:
                pool_layer(layer, False)
            pool_layer(3, True)
            pe.wait_ge(y_read, 4 * NCH - 1)
            pe.wait_ge(pooled_lo, 2 * 3 * NCH + 1)
            for q in range(CT):
                project_tile(bank[4 + q][:, 0:C], q, 0, (NCH - 1) % 2, w_proj[:, 3])
            pe.wait_ge(pooled_lo, 2 * 3 * NCH + 2)
            for q in range(CT):
                done = project_tile(bank[4 + q][:, 0:C], q, 1, (NCH - 1) % 2, w_proj[:, 3])
                done.then_inc(last_y_done, 1)

        @block.scalar
        def _(act):
            def convert(j):
                for h in range(2):
                    k = 2 * j + h
                    act.wait_ge(stage_in[k % STAGES], 16 * (k // STAGES + 1))
                    nc.scalar.activation(a8[:, j, h * (N // 2):(h + 1) * (N // 2)], stage[:, k % STAGES, :],
                                         ACT.Copy, accum_out=rowsum[:, j, h:h + 1], saturate=False) \
                        .then_inc(a8_made, 1)

            def copy_hT(i):
                act.wait_ge(hT_done, i + 1)
                if i > 0:
                    act.wait_ge(y0_done, i)
                nc.scalar.activation(hT[:, 0].rearrange("p k b n -> p (k b n)"), input_bank[:, :], ACT.Relu) \
                    .then_inc(hT_copied, 1)
                if i + 2 < T // 2:
                    act.dma_start(x_pairs[:, i % 2], x_in_pairs[i + 2]).then_inc(x_pair_in[i % 2], 16)

            for j in range(T):
                convert(j)
                if j == 0:
                    copy_hT(0)
                for u in copied_behind[j]:
                    act.wait_ge(partial_summed, u + 1)
                    if u >= 2:
                        act.wait_ge(partial_stored[u % 2], 16 * (u // 2))
                    nc.scalar.copy(partial_out[:, u % 2, :], partial_bank[:, :]).then_inc(partial_copied, 1)
                if j % 2 == 0 and j > 0:
                    copy_hT(j // 2)

            act.wait_ge(streamed, T)
            for ch in range(STREAMED):
                if ch == 2:
                    act.wait_ge(y_done, 1)
                for c in range(KT):
                    nc.scalar.copy(pooledT[:, ch % 2, c, :], acc_streamed(ch)[c][:, :]).then_inc(pooled_made, 1)

            def copy_pooled(ch):
                act.wait_ge(acc_done, ch - (STREAMED - 1))
                act.wait_ge(y_done, ch if ch == NCH - 1 else ch - 1)
                for c in range(KT):
                    nc.scalar.copy(pooledT[:, buffer_of(ch), c, :], acc(ch)[c][:, :]).then_inc(pooled_made, 1)

            def pooled_high(parity, n, src=None):
                act.wait_ge(y_done, n - 1)
                for c in range(KT):
                    nc.scalar.activation(pooled_parts[:, parity, 0, c, :], src[c] if src else acc(parity)[c][:, :],
                                         ACT.Copy, scale=pooled_unit[:, 1:2]).then_inc(pooled_hi, 1)

            def g_hi(layer, n):
                if layer == 3:
                    return
                if layer == 2:
                    act.wait_ge(tanh_in, n - (2 * NCH - 1))
                    nc.scalar.activation(update[:, :, :], update[:, :, :], ACT.Tanh).then_inc(tanh_done, 1)
                if layer == 0 and n < NCH - 1:
                    act.wait_ge(ln_made, n + 1)
                    for q in range(CT):
                        last = nc.scalar.activation(gfull[:, q, :], x[:, n % 2, q, :], ACT.Relu,
                                                    bias=ln_bias[:, q:q + 1], scale=ln_scale[:, q:q + 1])
                    last.then_inc(gfull_made, 1)
                act.wait_ge(gfull_made, n + 1)
                if layer > 0 or not isinstance(n, int) or n > 0:
                    act.wait_ge(g_spilled, n * 16 - layer * 16)
                nc.scalar.activation(g_out[:, :, 0, :], gfull[:, :, :], ACT.Relu).then_inc(hi_made, 1)

            for b in range(2):
                act.wait_ge(partial_stored[b], 16 * ((len(units) + 1 - b) // 2))
            copied_after = {0: 3, 1: 4, 2: 5, 4: 6, 5: 7}
            for ch in range(NCH):
                if ch == NCH - 2:
                    act.wait_ge(pooled_unit_made, 1)
                    act.wait_ge(partial_added, len(units))
                    pooled_high((NCH - 1) % 2, NCH - 1, [pooledT[:, buffer_of(NCH - 1), c, :] for c in range(KT)])
                g_hi(0, ch)
                if ch in copied_after:
                    copy_pooled(copied_after[ch])
            for layer in range(1, 4):
                if layer < 3:
                    act.wait_ge(g_in[NCH - 1], 16 * layer)
                with nc.scalar.Fori(0, NCH // 2) as pair:
                    for b in range(2):
                        n = pair * 2 + (layer * NCH + b)
                        act.wait_ge(acc_done, n - (STREAMED - 1))
                        pooled_high(b, n)
                        g_hi(layer, n)

        @block.vector
        def _(dve):
            class Steps:
                def __init__(self):
                    self.base, self.taken = 0, 0

                def after(self, ins, before_norm=False):
                    ins.then_inc(dve_step, 1)
                    self.taken += 1
                    if before_norm:
                        wait_past(dve, dve_step, self.base + self.taken)
                    else:
                        dve.wait_ge(dve_step, self.base + self.taken)

                def loop(self, start, stop, body, per_pass):
                    total = self.base + self.taken
                    with nc.vector.Fori(start, stop) as i:
                        self.base = (i - start) * per_pass + total
                        self.taken = 0
                        body(i)
                        assert self.taken == per_pass, (self.taken, per_pass)
                    self.base = 0
                    self.taken = total + per_pass * (stop - start)

            st = Steps()
            after = st.after
            V = nc.vector

            def rsqrt(dst, src, a, b):
                after(V.tensor_scalar(a.bitcast(I32), src.bitcast(I32), 1, None, ALU.logical_shift_right))
                after(V.tensor_scalar(dst.bitcast(I32), a.bitcast(I32), -1.0, float(0x5f3759df),
                                      ALU.mult, ALU.add))
                for _ in range(3):
                    after(V.tensor_tensor(a, dst, dst, ALU.mult))
                    after(V.scalar_tensor_tensor(b, a, -0.5, src, ALU.mult, ALU.mult))
                    after(V.scalar_tensor_tensor(dst, b, 1.5, dst, ALU.add, ALU.mult))

            RSQRT_STEPS = 11

            def norm_stats(tiles, n, var_out, factor=1.0):
                for q in range(n):
                    last = V.bn_stats(stats[:, q, :], tiles[:, q, :])
                after(last, before_norm=True)
                for q in range(n):
                    last = V.bn_aggr(mv[:, q, :], stats[:, q, :])
                after(last)
                after(V.tensor_scalar(var_out, mv[:, 0:n, 1], LN_EPS, factor, ALU.add, ALU.mult))

            def pair_step(i, parity, norm, weigh):
                if norm:
                    tiles = x_pairs[:, parity]
                    wait_past(dve, x_pair_in[parity], (i - parity) * 8 + 16)
                    norm_stats(tiles, 2, radicand[:, 2:4], H_SCALE ** -2)
                if weigh:
                    dve.wait_ge(hT_copied, i)
                    V.scalar_tensor_tensor(hT[:, 1].rearrange("p k b n -> p (k b n)"), input_bank[:, :], 0.0,
                                           hT[:, 0].rearrange("p k b n -> p (k b n)"), ALU.max, ALU.subtract) \
                        .then_inc(hT_low, 1)
                if weigh:
                    cols = bass.ds((i - 1) * 2, 2)
                    dve.wait_ge(a8_made, i * 4)
                    after(V.scalar_tensor_tensor(radicand[:, 0:2], rowsum[:, cols, 0], 1.0, rowsum[:, cols, 1],
                                                 ALU.add, ALU.add))
                    V.tensor_copy(deg1[:, cols], radicand[:, 0:2])
                used = slice(0 if weigh else 2, 4 if norm else 2)
                rsqrt(root[:, used], radicand[:, used], newton_a[:, used], newton_b[:, used])
                if norm:
                    for b in range(2):
                        last = V.tensor_scalar(tiles[:, b, :], tiles[:, b, :], mv[:, b, 0:1],
                                               root[:, 2 + b:3 + b], ALU.subtract, ALU.mult)
                    last.then_inc(h_made, 1)
                if weigh:
                    V.tensor_copy(dinv1[:, cols], root[:, 0:2])
                    after(V.tensor_scalar(y0_scale[:, :], root[:, 0:2], 2.0 / C / H_SCALE, None, ALU.mult))
                    dve.wait_ge(y0_done, i)
                    for b in range(2):
                        last = V.tensor_scalar(y0[:, b, :], input_bank[:, b * C:(b + 1) * C],
                                               y0_scale[:, b:b + 1], None, ALU.mult)
                    after(last)
                    pair = g[:, cols]
                    after(V.tensor_copy(pair[:, :, 0, :], y0[:, :, :]))
                    V.tensor_tensor(pair[:, :, 1, :], y0[:, :, :], pair[:, :, 0, :], ALU.subtract) \
                        .then_inc(g0_made, 1)
                    dve.wait_ge(g0_made, i)

            pair_step(0, 0, True, False)

            dve.wait_ge(w_in_loaded, 16 * 2)
            V.tensor_reduce(wmax_part[:, 0:1], w_in_raw.rearrange("p w k n -> p (w k n)"), AX.X, ALU.max,
                            apply_absolute_value=True).then_inc(wmax_part_made, 1)
            dve.wait_ge(wmax_made, 1)
            after(V.tensor_scalar(wmax[:, 0:1], wmax[:, 0:1], C * 2.0 ** -15, 1e-30, ALU.mult, ALU.max))
            after(V.reciprocal(wmax[:, 1:2], wmax[:, 0:1]))
            after(V.tensor_scalar(wmax[:, 1:2], wmax[:, 1:2], C / 2, None, ALU.mult))
            after(V.tensor_scalar(w_in[:, :, 0], w_in_raw[:, :], wmax[:, 1:2], None, ALU.mult))
            V.scalar_tensor_tensor(w_in[:, :, 1], w_in_raw[:, :], wmax[:, 1:2], w_in[:, :, 0],
                                   ALU.mult, ALU.subtract).then_inc(w_in_made, 1)

            dve.wait_ge(h_made, 1)
            pair_step(1, 1, True, True)
            st.loop(1, T // 4, lambda m: [pair_step(m * 2 + b, b, True, True) for b in range(2)],
                    2 * (3 + 1 + RSQRT_STEPS + 3))
            pair_step(T // 2, 0, False, True)

            after(V.tensor_scalar(deg[:, :], deg1[:, :], -1.0, 1.0, ALU.add, ALU.max))
            V.tensor_reduce(maxes_part[:, 3:4], deg[:, :], AX.X, ALU.max).then_inc(maxes_part_made, 1)
            dve.wait_ge(proj_in, 16 * 3)
            V.tensor_reduce(maxes_part[:, 0:3], w_raw.rearrange("p l k n -> p l (k n)"), AX.X, ALU.max,
                            apply_absolute_value=True).then_inc(maxes_part_made, 1)

            V.tensor_scalar(out_scale[:, 0, :], dinv1[:, :], wmax[:, 0:1], None, ALU.mult)
            rsqrt(dinv[:, :], deg[:, :], newton_a[:, :], newton_b[:, :])
            V.tensor_scalar(out_scale[:, 1, :], dinv[:, :], 1.0 / G_SCALE, None, ALU.mult)
            V.tensor_scalar(out_scale[:, 2, :], dinv1[:, :], 1.0 / G_SCALE, None, ALU.mult)
            after(V.reciprocal(newton_a[:, :], deg[:, :]))
            V.tensor_scalar(out_scale[:, 3, :], newton_a[:, :], 1.0 / G_SCALE, None, ALU.mult)
            V.tensor_scalar(g_scale[:, 1, :], dinv[:, :], G_SCALE, None, ALU.mult)
            V.tensor_scalar(g_scale[:, 2, :], dinv1[:, :], G_SCALE, None, ALU.mult)
            V.memset(g_scale[:, 3, :], G_SCALE)
            after(V.tensor_copy(deg_bits[:, :], deg[:, :]))
            after(V.tensor_scalar(deg_bits[:, :], deg_bits[:, :], 1, None, ALU.bitwise_and))
            V.tensor_copy(deg_odd[:, :], deg_bits[:, :]).then_inc(odd_made, 1)
            dve.wait_ge(odd_made, 1)
            after(V.tensor_tensor(deg_even[:, :], deg[:, :], deg_odd[:, :], ALU.subtract))

            after(V.memset(w_proj[:, 0], 0.0))
            for k in range(KT):
                V.tensor_copy(w_proj[:, 0, 0, k, k * P:(k + 1) * P], ident[:, :])
            dve.wait_ge(maxes_made, 1)
            V.tensor_scalar(w_unit[:, 0, :], maxes[:, 0:3], 2.0 ** -14, 1e-30, ALU.mult, ALU.max)
            after(V.tensor_scalar(pooled_unit[:, 0:1], maxes[:, 3:4], 1.0, 2.0, ALU.add, ALU.mult))
            V.reciprocal(pooled_unit[:, 1:2], pooled_unit[:, 0:1]).then_inc(pooled_unit_made, 1)
            after(V.reciprocal(w_unit[:, 1, :], w_unit[:, 0, :]))
            for l in range(3):
                V.tensor_scalar(out_scale[:, l + 1, :], out_scale[:, l + 1, :], w_unit[:, 0, l:l + 1],
                                pooled_unit[:, 0:1], ALU.mult, ALU.mult)
                last = V.tensor_scalar(w_proj[:, l + 1, 0], w_raw[:, l], w_unit[:, 1, l:l + 1], None, ALU.mult)
            V.tensor_scalar(out_scale[:, 0, T - CT:], out_scale[:, 0, T - CT:], pooled_unit[:, 0:1], None, ALU.mult)
            after(last)
            for l in range(3):
                last = V.scalar_tensor_tensor(w_proj[:, l + 1, 1], w_raw[:, l], w_unit[:, 1, l:l + 1],
                                              w_proj[:, l + 1, 0], ALU.mult, ALU.subtract)
            last.then_inc(w_proj_made, 1)
            dve.wait_ge(w_proj_made, 1)
            dve.wait_ge(bias_in, 16 * 4)

            def make_diag(ch, parity):
                for q in range(CT):
                    last = V.tensor_scalar(diag[:, parity, q, :], ident[:, :],
                                           deg_even[:, bass.ds(ch * CT + q, 1)], None, ALU.mult)
                last.then_inc(diag_made, 1)

            def scale_y(layer, ch, parity):
                n = ch + layer * NCH
                dve.wait_ge(y_done, n + 1)
                for q in range(CT):
                    last = V.scalar_tensor_tensor(update[:, q, :], y_of(parity, q),
                                                  out_scale[:, layer, bass.ds(ch * CT + q, 1)],
                                                  bias[:, layer, :], ALU.mult, ALU.add)
                last.then_inc(y_read, 1)
                dve.wait_ge(y_read, n + 1)
                if layer == 0:
                    after(V.scalar_tensor_tensor(update[:, :, :], update[:, :, :], LEAK, update[:, :, :],
                                                 ALU.mult, ALU.max))

            def new_x(layer, ch, parity):
                n = ch + layer * NCH
                xs = x[:, parity]
                if layer == 2:
                    V.tensor_copy(stats[:, 0, 0:1], update[:, CT - 1, 0:1]).then_inc(tanh_in, 1)
                    dve.wait_ge(tanh_done, ch + 1)
                dve.wait_ge(x_in_sb[parity], (n - parity) * 8 + 16)
                if layer == 3:
                    V.scalar_tensor_tensor(xs, update[:, :, :], 0.0, xs, ALU.max, ALU.add).then_inc(x_made, 1)
                    dve.wait_ge(x_made, n + 1)
                    return
                V.tensor_tensor(xs, update[:, :, :], xs, ALU.add).then_inc(x_made, 1)
                wait_past(dve, x_made, n + 1)
                norm_stats(xs, CT, radicand[:, 0:CT])
                rsqrt(root[:, 0:CT], radicand[:, 0:CT], newton_a[:, 0:CT], newton_b[:, 0:CT])
                after(V.tensor_tensor(ln_scale[:, :], root[:, 0:CT], g_scale[:, layer + 1, bass.ds(ch * CT, CT)],
                                      ALU.mult))
                if layer == 0 and ch < NCH - 1:
                    V.scalar_tensor_tensor(ln_bias[:, :], mv[:, :, 0], -1.0, ln_scale[:, :],
                                           ALU.mult, ALU.mult).then_inc(ln_made, 1)
                    return
                for q in range(CT):
                    last = V.tensor_scalar(gfull[:, q, :], xs[:, q, :], mv[:, q, 0:1],
                                           ln_scale[:, q:q + 1], ALU.subtract, ALU.mult)
                last.then_inc(gfull_made, 1)

            def g_lo(layer, ch):
                n = ch + layer * NCH
                dve.wait_ge(gfull_made, n + 1)
                dve.wait_ge(hi_made, n + 1)
                V.scalar_tensor_tensor(g_out[:, :, 1, :], gfull[:, :, :], 0.0, g_out[:, :, 0, :],
                                       ALU.max, ALU.subtract).then_inc(g_made, 1)
                dve.wait_ge(g_made, n + 1)

            def pooled_low(ch, parity, n, src=None):
                for c in range(KT):
                    dve.wait_ge(pooled_hi, n * 2 - (2 * NCH - 3 - c))
                    V.scalar_tensor_tensor(pooled_parts[:, parity, 1, c, :], src[c] if src else acc(ch)[c][:, :],
                                           pooled_unit[:, 1:2], pooled_parts[:, parity, 0, c, :],
                                           ALU.mult, ALU.subtract).then_inc(pooled_lo, 1)

            def finish(layer, ch, parity):
                pooled_low(parity, parity, ch + layer * NCH)
                scale_y(layer, ch, parity)
                new_x(layer, ch, parity)
                if layer < 3:
                    g_lo(layer, ch)

            scale_y(0, 0, 0)
            for ch in range(NCH):
                new_x(0, ch, ch % 2)
                if ch + 2 < NCH:
                    scale_y(0, ch + 1, (ch + 1) % 2)
                if ch + 2 == NCH:
                    pooled_low(ch + 1, (ch + 1) % 2, ch + 1, [pooledT[:, buffer_of(ch + 1), c, :] for c in range(KT)])
                g_lo(0, ch)
                if ch + 2 == NCH:
                    scale_y(0, ch + 1, (ch + 1) % 2)
            norm_steps = 3 + RSQRT_STEPS + 1
            finish_steps = [None, norm_steps, norm_steps, 0]

            for layer in range(1, 4):
                def pair_of_chunks(pair):
                    for b in range(2):
                        ch = pair * 2 + b
                        if layer == 3:
                            dve.wait_ge(acc_done, ch + (3 * NCH + 1 - STREAMED))
                        finish(layer, ch, b)
                        if layer == 3:
                            make_diag_ahead(ch, b)

                def make_diag_ahead(ch, b):
                    make_diag(ch + 2, b)

                if layer < 3:
                    st.loop(0, NCH // 2, pair_of_chunks, 2 * finish_steps[layer])
                else:
                    for b in range(2):
                        make_diag(b, b)
                    st.loop(0, NCH // 2 - 1, pair_of_chunks, 0)
                    finish(3, NCH - 2, 0)
            pooled_low(NCH - 1, (NCH - 1) % 2, 4 * NCH - 1)
            dve.wait_ge(x_in_sb[1], 16 * 4 * (NCH // 2))
            for q in range(CT + 1):
                if q < CT:
                    dve.wait_ge(last_y_done, q + 1)
                    V.scalar_tensor_tensor(update[:, q, :], bank[4 + q][:, 0:C],
                                           out_scale[:, 3, T - CT + q:T - CT + q + 1], bias[:, 3, :],
                                           ALU.mult, ALU.add).then_inc(last_scaled, 1)
                if q > 0:
                    dve.wait_ge(last_scaled, q)
                    V.scalar_tensor_tensor(x[:, 1, q - 1, :], update[:, q - 1, :], 0.0, x[:, 1, q - 1, :],
                                           ALU.max, ALU.add).then_inc(last_x_made, 1)


_INS = ["x", "adj", "L0_gnn_weightr", "L0_gnn_weightd", "L0_gnn_bias", "L1_gnn_W", "L1_gnn_b",
        "L2_gnn_W", "L2_gnn_b", "L3_gnn_W", "L3_gnn_b"]


def kernel(**inputs):
    import numpy as _np
    import concourse.bacc as _bacc
    from concourse import mybir as _mybir
    from concourse.bass_utils import run_bass_kernel_spmd as _run

    nc = _bacc.Bacc("TRN2", target_bir_lowering=False, num_devices=1)
    arrays, args = {}, []
    for name in _INS:
        a = _np.asarray(inputs[name])
        if name in ("L1_gnn_W", "L2_gnn_W"):
            a = a.T
        a = _np.ascontiguousarray(a)
        arrays[f"in_{name}"] = a
        args.append(nc.dram_tensor(f"in_{name}", a.shape, _mybir.dt.from_np(a.dtype), kind="ExternalInput").ap())
    out = nc.dram_tensor("out", (4096, 256), _mybir.dt.float32, kind="ExternalOutput").ap()
    build(nc, *args, out)
    r = _run(nc, [arrays], core_ids=[0])
    return r.results[0]["out"]
```
